# Optimizing a Trainium2 kernel written in Bass

```python
import numpy as np
import jax
import jax.numpy as jnp

def _softmax(x, axis=-1):
    return jax.nn.softmax(x, axis=axis)

def _gelu(x):
    return jax.nn.gelu(x, approximate=True)

def _silu(x):
    return jax.nn.silu(x)

def _sigmoid(x):
    return jax.nn.sigmoid(x)

def _layernorm(x, axis=-1, eps=1e-05):
    m = jnp.mean(x, axis=axis, keepdims=True)
    v = jnp.var(x, axis=axis, keepdims=True)
    return (x - m) / jnp.sqrt(v + eps)

def _scatter_add(tgt, idx, src, axis=0):
    return tgt.at[idx].add(src)

def _segment_sum(src, seg, n):
    return jax.ops.segment_sum(src, seg, n)
kernel_name = 'mk_cond_resid_d1_seqx_r2_ea1cd0'

def setup_inputs(seed: int=0):
    np.random.seed(seed)
    _w = jnp.asarray

    def _rec_inputs():
        import jax
        import jax.numpy as jnp
        _rk = jax.random.key(seed)
        x = 7.22e-05 + 1 * jax.random.normal(jax.random.fold_in(_rk, 1), (2, 2048, 512), jnp.float32)
        _lenS = 2048 - jax.random.randint(jax.random.fold_in(_rk, 7), (2,), 0, max(1, 2048 // 4) + 1, jnp.int32)
        _lenS2 = 2048 - jax.random.randint(jax.random.fold_in(_rk, 8), (2,), 0, max(1, 2048 // 4) + 1, jnp.int32)
        cond_256 = 0.000887014 + 1.03683 * jax.random.normal(jax.random.fold_in(_rk, 11), (2, 128), jnp.float32)
        return (x, cond_256)
    x, cond_256 = _rec_inputs()

    def _L0_cond_setup():
        import jax, jax.numpy as jnp
        import numpy as np
        D_MODEL = 512
        D_T = 128
        N_HEADS = 16
        HIDDEN = 4 * D_MODEL
        EPS = 1e-06

        def _tc_rmsnorm(x, t, gw, gb, bw, bb):
            g = (t @ gw.T + gb)[:, None, :]
            b = (t @ bw.T + bb)[:, None, :]
            inv_rms = jax.lax.rsqrt(jnp.mean(x * x, axis=-1, keepdims=True) + EPS)
            return g * x * inv_rms + b

        def _attention(x, Wq, Wk, Wv, Wo):
            B, L, D = x.shape
            H = N_HEADS
            dh = D // H
            scale = np.sqrt(dh).astype(np.float32)
            q = (x @ Wq.T).reshape(B, L, H, dh)
            k = (x @ Wk.T).reshape(B, L, H, dh)
            v = (x @ Wv.T).reshape(B, L, H, dh)
            attn = jnp.einsum('blhd,bmhd->bhlm', q, k) / scale
            p = jax.nn.softmax(attn, axis=-1)
            o = jnp.einsum('bhlm,bmhd->blhd', p, v).reshape(B, L, D)
            return o @ Wo.T

        def _swiglu(x, gate_w, hid_w, out_w):
            return jax.nn.silu(x @ gate_w.T) * (x @ hid_w.T) @ out_w.T
        key = jax.random.key(seed)
        ks = jax.random.split(key, 20)
        B, L = (8, 512)
        s_d = 1.0 / np.sqrt(D_MODEL)
        s_t = 1.0 / np.sqrt(D_T)
        s_h = 1.0 / np.sqrt(HIDDEN)
        return {'x': jax.random.normal(ks[0], (B, L, D_MODEL), jnp.float32), 't': jax.random.normal(ks[1], (B, D_T), jnp.float32), 'Wq': jax.random.normal(ks[2], (D_MODEL, D_MODEL), jnp.float32) * s_d, 'Wk': jax.random.normal(ks[3], (D_MODEL, D_MODEL), jnp.float32) * s_d, 'Wv': jax.random.normal(ks[4], (D_MODEL, D_MODEL), jnp.float32) * s_d, 'Wo': jax.random.normal(ks[5], (D_MODEL, D_MODEL), jnp.float32) * s_d, 'g1w': jax.random.normal(ks[6], (D_MODEL, D_T), jnp.float32) * s_t, 'g1b': jnp.ones((D_MODEL,), jnp.float32), 'b1w': jax.random.normal(ks[7], (D_MODEL, D_T), jnp.float32) * s_t, 'b1b': jnp.zeros((D_MODEL,), jnp.float32), 'g2w': jax.random.normal(ks[8], (D_MODEL, D_T), jnp.float32) * s_t, 'g2b': jnp.ones((D_MODEL,), jnp.float32), 'b2w': jax.random.normal(ks[9], (D_MODEL, D_T), jnp.float32) * s_t, 'b2b': jnp.zeros((D_MODEL,), jnp.float32), 'gate_w': jax.random.normal(ks[10], (HIDDEN, D_MODEL), jnp.float32) * s_d, 'hid_w': jax.random.normal(ks[11], (HIDDEN, D_MODEL), jnp.float32) * s_d, 'out_w': jax.random.normal(ks[12], (D_MODEL, HIDDEN), jnp.float32) * s_h}
    _L0_cond_all = _L0_cond_setup()
    _L0_cond_in = {k: v for k, v in _L0_cond_all.items() if k in ('Wq', 'Wk', 'Wv', 'Wo', 'g1w', 'g1b', 'b1w', 'b1b', 'g2w', 'g2b', 'b2w', 'b2b', 'gate_w', 'hid_w', 'out_w')}
    del _L0_cond_all
    return {'x': x, 'cond_256': cond_256, 'L0_cond_Wq': _L0_cond_in['Wq'], 'L0_cond_Wk': _L0_cond_in['Wk'], 'L0_cond_Wv': _L0_cond_in['Wv'], 'L0_cond_Wo': _L0_cond_in['Wo'], 'L0_cond_g1w': _L0_cond_in['g1w'], 'L0_cond_g1b': _L0_cond_in['g1b'], 'L0_cond_b1w': _L0_cond_in['b1w'], 'L0_cond_b1b': _L0_cond_in['b1b'], 'L0_cond_g2w': _L0_cond_in['g2w'], 'L0_cond_g2b': _L0_cond_in['g2b'], 'L0_cond_b2w': _L0_cond_in['b2w'], 'L0_cond_b2b': _L0_cond_in['b2b'], 'L0_cond_gate_w': _L0_cond_in['gate_w'], 'L0_cond_hid_w': _L0_cond_in['hid_w'], 'L0_cond_out_w': _L0_cond_in['out_w']}

def reference(x, cond_256, L0_cond_Wq, L0_cond_Wk, L0_cond_Wv, L0_cond_Wo, L0_cond_g1w, L0_cond_g1b, L0_cond_b1w, L0_cond_b1b, L0_cond_g2w, L0_cond_g2b, L0_cond_b2w, L0_cond_b2b, L0_cond_gate_w, L0_cond_hid_w, L0_cond_out_w):
    import jax
    import jax.numpy as jnp

    def _L0_cond_ref(x, t, Wq, Wk, Wv, Wo, g1w, g1b, b1w, b1b, g2w, g2b, b2w, b2b, gate_w, hid_w, out_w):
        import jax, jax.numpy as jnp
        import numpy as np
        D_MODEL = 512
        D_T = 128
        N_HEADS = 16
        HIDDEN = 4 * D_MODEL
        EPS = 1e-06

        def _tc_rmsnorm(x, t, gw, gb, bw, bb):
            g = (t @ gw.T + gb)[:, None, :]
            b = (t @ bw.T + bb)[:, None, :]
            inv_rms = jax.lax.rsqrt(jnp.mean(x * x, axis=-1, keepdims=True) + EPS)
            return g * x * inv_rms + b

        def _attention(x, Wq, Wk, Wv, Wo):
            B, L, D = x.shape
            H = N_HEADS
            dh = D // H
            scale = np.sqrt(dh).astype(np.float32)
            q = (x @ Wq.T).reshape(B, L, H, dh)
            k = (x @ Wk.T).reshape(B, L, H, dh)
            v = (x @ Wv.T).reshape(B, L, H, dh)
            attn = jnp.einsum('blhd,bmhd->bhlm', q, k) / scale
            p = jax.nn.softmax(attn, axis=-1)
            o = jnp.einsum('bhlm,bmhd->blhd', p, v).reshape(B, L, D)
            return o @ Wo.T

        def _swiglu(x, gate_w, hid_w, out_w):
            return jax.nn.silu(x @ gate_w.T) * (x @ hid_w.T) @ out_w.T
        x = x + _attention(_tc_rmsnorm(x, t, g1w, g1b, b1w, b1b), Wq, Wk, Wv, Wo)
        return x + _swiglu(_tc_rmsnorm(x, t, g2w, g2b, b2w, b2b), gate_w, hid_w, out_w)
    x = x + _L0_cond_ref(x, cond_256, L0_cond_Wq, L0_cond_Wk, L0_cond_Wv, L0_cond_Wo, L0_cond_g1w, L0_cond_g1b, L0_cond_b1w, L0_cond_b1b, L0_cond_g2w, L0_cond_g2b, L0_cond_b2w, L0_cond_b2b, L0_cond_gate_w, L0_cond_hid_w, L0_cond_out_w)
    return x

_drawn_inputs = setup_inputs


def setup_inputs(seed=0):
    import zlib

    import numpy as np

    out = dict(_drawn_inputs(seed))
    spreads = {'L0_cond_g1b': (1.0, 0.2),
     'L0_cond_b1b': (0.0, 0.1),
     'L0_cond_g2b': (1.0, 0.2),
     'L0_cond_b2b': (0.0, 0.1)}
    factors = {}
    for name, (base, spread) in spreads.items():
        noise = np.random.default_rng([zlib.crc32(name.encode()), seed]).standard_normal(out[name].shape)
        drawn = base * np.exp(spread * noise) if base else spread * noise
        out[name] = jnp.asarray(drawn.astype(out[name].dtype))
    for name, factor in factors.items():
        out[name] = (out[name] * factor).astype(out[name].dtype)
    return out
```

```python
from contextlib import ExitStack

import concourse.bass as bass
from concourse import mybir

F32 = mybir.dt.float32
F32R = mybir.dt.float32r
ALU = mybir.AluOpType
ACT = mybir.ActivationFunctionType
AX_X = mybir.AxisListType.X

P = 128
B, L, D, HEADS, HIDDEN = 2, 2048, 512, 16, 2048
DH = D // HEADS
TOKENS = B * L
CH = 512
CHUNKS = TOKENS // CH
CPB = L // CH
KT = D // P
HG = P // DH
GROUPS = HEADS // HG
EPS = 1e-6
SCALE = 1.0 / float(DH) ** 0.5
PASSES = ((0, 0), (0, 1), (1, 0))
NORM = 3 + KT


class Rig:

    def __init__(self, nc, ctx, tag):
        self.nc, self.ctx, self.tag = nc, ctx, tag

    def sb(self, name, shape, dt=F32):
        return self.ctx.enter_context(self.nc.sbuf_tensor(f"{self.tag}_{name}", shape, dt))

    def ps(self, name, shape, dt=F32):
        return self.ctx.enter_context(self.nc.psum_tensor(f"{self.tag}_{name}", shape, dt))

    def sem(self, name):
        return self.ctx.enter_context(self.nc.semaphore(f"{self.tag}_{name}"))


def project(nc, xT, cT, wT, modT, mod_bias, ones_in, qk_scr, v_scr, mod):
    QK = 2 * GROUPS
    TILES = QK + CH // P
    BANKS = 6
    SLOTS = 4
    VSLOTS = 2
    with ExitStack() as ctx:
        rig = Rig(nc, ctx, "p1")
        w_raw = rig.sb("w_raw", [P, 3, KT, D])
        w_part = rig.sb("w_part", [P, 2, 3, KT, D], F32R)
        mod_w = rig.sb("mod_w", [P, 4, D])
        cond = rig.sb("cond", [P, B])
        bias = rig.sb("bias", [P, B, 4, KT])
        gb = rig.sb("gb", [P, 2, KT])
        ones = rig.sb("ones", [P, P])
        xc = rig.sb("xc", [P, 2, KT, CH])
        sq = rig.sb("sq", [P, KT, CH])
        rms = rig.sb("rms", [P, CH])
        inv = rig.sb("inv", [P, CH])
        h = rig.sb("h", [P, 2, 2, KT, CH], F32R)
        out_qk = rig.sb("out_qk", [P, SLOTS, 2, CH])
        out_v = rig.sb("out_v", [P, VSLOTS, D])
        tile = rig.ps("tile", [P, BANKS, CH])
        ss = rig.ps("ss", [P, CH])
        mod_ps = rig.ps("mod_ps", [P, B, 4, KT])

        consts_in = rig.sem("consts_in")
        weights_in = rig.sem("weights_in")
        weight_hi = rig.sem("weight_hi")
        weights_split = rig.sem("weights_split")
        mod_sums = rig.sem("mod_sums")
        mod_ready = rig.sem("mod_ready")
        x_in = [rig.sem(f"x_in{i}") for i in range(2)]
        sq_ready = rig.sem("sq_ready")
        ss_ready = rig.sem("ss_ready")
        rms_ready = rig.sem("rms_ready")
        norm_step = rig.sem("norm_step")
        h_hi = rig.sem("h_hi")
        h_ready = rig.sem("h_ready")
        tile_ready = rig.sem("tile_ready")
        tile_hi = rig.sem("tile_hi")
        tile_free = rig.sem("tile_free")
        qk_stored = [rig.sem(f"qk_stored{i}") for i in range(SLOTS)]
        v_stored = [rig.sem(f"v_stored{i}") for i in range(VSLOTS)]

        with nc.Block() as block:

            @block.gpsimd
            def _(pool):
                def load_x(c, par):
                    pool.dma_start(xc[:, par, :, :], xT[:, c, :, :].rearrange("k p t -> p k t")
                                   ).then_inc(x_in[par], 16)

                load_x(0, 0)
                pool.dma_start(ones[:, :], ones_in[:, :]).then_inc(consts_in, 16)
                pool.dma_start(cond[:, :], cT[:, :]).then_inc(consts_in, 16)
                pool.dma_start(bias[:, :, :, :], mod_bias[:, :, :, :]).then_inc(consts_in, 16)
                pool.dma_start(mod_w[:, :, :], modT[:, :, :]).then_inc(consts_in, 16)
                load_x(1, 1)
                with pool.Fori(1, CHUNKS // 2) as it:
                    for par in range(2):
                        c = it * 2 + par
                        pool.wait_ge(h_ready, c - 1)
                        load_x(c, par)

            @block.sync
            def _(sp):
                for j in range(3):
                    sp.dma_start(w_raw[:, j, :, :], wT[j].rearrange("(k p) n -> p k n", p=P)
                                 ).then_inc(weights_in, 16)
                with sp.Fori(0, CHUNKS) as c:
                    for k in range(TILES):
                        sp.wait_ge(tile_free, c * TILES + BANKS + k + 1)
                        if k < QK:
                            for part in range(2):
                                sp.dma_start(qk_scr[k % 2, part, k // 2, c // CPB, c % CPB, :, :],
                                             out_qk[:, k % SLOTS, part, :]
                                             ).then_inc(qk_stored[k % SLOTS], 16)
                        else:
                            j = k - QK
                            sp.dma_start(v_scr[c // CPB, c % CPB * (CH // P) + j, :, :], out_v[:, j % VSLOTS, :]
                                         ).then_inc(v_stored[j % VSLOTS], 16)
                for s in range(SLOTS):
                    sp.wait_ge(qk_stored[s], 32 * (QK // SLOTS) * CHUNKS)
                for s in range(VSLOTS):
                    sp.wait_ge(v_stored[s], 16 * (TILES - QK) // VSLOTS * CHUNKS)

            @block.scalar
            def _(act):
                def square(c, par, x_count):
                    act.wait_ge(x_in[par], x_count)
                    act.wait_ge(ss_ready, c)
                    act.activation(sq[:, :, :], xc[:, par, :, :], ACT.Square).then_inc(sq_ready, 1)

                def root(c):
                    act.wait_ge(ss_ready, c + 1)
                    act.activation(rms[:, :], ss[:, :], ACT.Sqrt, scale=1.0 / D, bias=EPS
                                   ).then_inc(rms_ready, 1)

                def norm_hi(c, par):
                    act.wait_ge(norm_step, (c + 1) * NORM)
                    act.activation(h[:, par, 0, :, :], xc[:, par, :, :], ACT.Copy
                                   ).then_inc(h_hi, 1)

                def chunk(c, par, x_count, norm_next):
                    if norm_next:
                        square(c + 1, 1 - par, x_count)
                    for k in range(QK):
                        act.wait_ge(tile_ready, c * TILES + k + 1)
                        act.wait_ge(qk_stored[k % SLOTS],
                                    c * (32 * (QK // SLOTS)) + 32 * (k // SLOTS))
                        act.activation(out_qk[:, k % SLOTS, 0, :].bitcast(F32R),
                                       tile[:, k % BANKS, :], ACT.Copy).then_inc(tile_hi, 1)
                        if norm_next and k == 3:
                            root(c + 1)
                    if norm_next:
                        norm_hi(c + 1, 1 - par)

                act.wait_ge(x_in[0], 16)
                act.activation(sq[:, :, :], xc[:, 0, :, :], ACT.Square).then_inc(sq_ready, 1)
                act.wait_ge(weights_in, 48)
                for j in range(3):
                    act.activation(w_part[:, 0, j, :, :], w_raw[:, j, :, :], ACT.Copy
                                   ).then_inc(weight_hi, 1)
                root(0)
                norm_hi(0, 0)
                with act.Fori(0, CHUNKS // 2 - 1) as it:
                    chunk(it * 2, 0, it * 16 + 16, True)
                    chunk(it * 2 + 1, 1, it * 16 + 32, True)
                chunk(CHUNKS - 2, 0, 16 * (CHUNKS // 2), True)
                chunk(CHUNKS - 1, 1, None, False)

            @block.vector
            def _(dve):
                dve.sem_inc(tile_free, BANKS)

                def norm(c, par):
                    done = c * NORM
                    dve.wait_ge(norm_step, done)
                    dve.tensor_scalar(gb[:, :, :], mod[:, c // CPB, 0:2, :], 1.0, None, ALU.mult
                                      ).then_inc(norm_step, 1)
                    dve.wait_ge(rms_ready, c + 1)
                    dve.reciprocal(inv[:, :], rms[:, :]).then_inc(norm_step, 1)
                    dve.wait_ge(norm_step, done + 2)
                    dve.tensor_tensor(xc[:, par, :, :], xc[:, par, :, :],
                                      inv[:, :].unsqueeze(1).broadcast_to([P, KT, CH]),
                                      ALU.mult).then_inc(norm_step, 1)
                    dve.wait_ge(norm_step, done + 3)
                    for k in range(KT):
                        dve.tensor_scalar(xc[:, par, k, :], xc[:, par, k, :], gb[:, 0, k:k + 1],
                                          gb[:, 1, k:k + 1], ALU.mult, ALU.add
                                          ).then_inc(norm_step, 1)

                def norm_lo(c, par):
                    dve.wait_ge(h_hi, c + 1)
                    dve.tensor_tensor(h[:, par, 1, :, :], xc[:, par, :, :],
                                      h[:, par, 0, :, :].bitcast(F32), ALU.subtract
                                      ).then_inc(h_ready, 1)

                def chunk(c, par, norm_next):
                    for k in range(QK):
                        dve.wait_ge(tile_hi, c * QK + k + 1)
                        dve.tensor_tensor(out_qk[:, k % SLOTS, 1, :].bitcast(F32R),
                                          tile[:, k % BANKS, :], out_qk[:, k % SLOTS, 0, :],
                                          ALU.subtract).then_inc(tile_free, 1)
                        if norm_next and k == 3:
                            norm(c + 1, 1 - par)
                    if norm_next:
                        norm_lo(c + 1, 1 - par)
                    for k in range(QK, TILES):
                        j = k - QK
                        dve.wait_ge(tile_ready, c * TILES + k + 1)
                        dve.wait_ge(v_stored[j % VSLOTS],
                                    c * (16 * (TILES - QK) // VSLOTS) + 16 * (j // VSLOTS))
                        dve.tensor_copy(out_v[:, j % VSLOTS, :], tile[:, k % BANKS, :]
                                        ).then_inc(tile_free, 1)

                dve.wait_ge(mod_sums, 1)
                dve.tensor_tensor(mod[:, :, :, :], mod_ps[:, :, :, :], bias[:, :, :, :], ALU.add
                                  ).then_inc(mod_ready, 1)
                dve.wait_ge(mod_ready, 1)
                for j in range(3):
                    dve.wait_ge(weight_hi, j + 1)
                    dve.tensor_tensor(w_part[:, 1, j, :, :], w_raw[:, j, :, :],
                                      w_part[:, 0, j, :, :].bitcast(F32), ALU.subtract
                                      ).then_inc(weights_split, 1)
                norm(0, 0)
                norm_lo(0, 0)
                with dve.Fori(0, CHUNKS // 2 - 1) as it:
                    chunk(it * 2, 0, True)
                    chunk(it * 2 + 1, 1, True)
                chunk(CHUNKS - 2, 0, True)
                chunk(CHUNKS - 1, 1, False)

            @block.tensor
            def _(pe):
                def sum_squares(c):
                    pe.wait_ge(sq_ready, c + 1)
                    pe.wait_ge(rms_ready, c)
                    for k in range(KT):
                        mm = pe.matmul(ss[:, :], ones[:, :], sq[:, k, :], start=(k == 0),
                                       stop=(k == KT - 1))
                    mm.then_inc(ss_ready, 1)

                def chunk(c, par, norm_next):
                    pe.wait_ge(h_ready, c + 1)
                    for k in range(TILES):
                        pe.wait_ge(tile_free, c * TILES + k + 1)
                        n = 0
                        for kt in range(KT):
                            for stat, mov in PASSES:
                                if k < QK:
                                    g = k // 2
                                    lhs = w_part[:, stat, k % 2, kt, g * P:(g + 1) * P]
                                    rhs = h[:, par, mov, kt, :]
                                else:
                                    j = k - QK
                                    lhs = h[:, par, stat, kt, j * P:(j + 1) * P]
                                    rhs = w_part[:, mov, 2, kt, :]
                                mm = pe.matmul(tile[:, k % BANKS, :], lhs, rhs, start=(n == 0),
                                               stop=(n == 3 * KT - 1))
                                n += 1
                        mm.then_inc(tile_ready, 1)
                        if norm_next and k == 1:
                            sum_squares(c + 1)

                pe.wait_ge(consts_in, 64)
                for v in range(4):
                    for kt in range(KT):
                        mm = pe.matmul(mod_ps[:, :, v, kt], mod_w[:, v, kt * P:(kt + 1) * P],
                                       cond[:, :], start=True, stop=True)
                mm.then_inc(mod_sums, 1)
                sum_squares(0)
                pe.wait_ge(weights_split, 3)
                with pe.Fori(0, CHUNKS // 2 - 1) as it:
                    chunk(it * 2, 0, True)
                    chunk(it * 2 + 1, 1, True)
                chunk(CHUNKS - 2, 0, True)
                chunk(CHUNKS - 1, 1, False)


def attend(nc, qk_scr, v_scr, o_scr, ones_in, ident_in):
    STAGES = B * GROUPS * CPB
    MT = L // P
    QT = CH // P
    KC = L // CH
    ROWS = 3 * DH
    AUG = ROWS + 2
    MAXMM = HG * QT * KC
    SLOT = MAXMM + 2
    UNITS = 8
    UPS = 2 * MT
    KV_DMAS = 3 * HG + 1
    with ExitStack() as ctx:
        rig = Rig(nc, ctx, "p2")
        q_stat = rig.sb("q_stat", [ROWS, HG, CH], F32R)
        q_mov = rig.sb("q_mov", [AUG, 2, HG, CH], F32R)
        k_mov = rig.sb("k_mov", [ROWS, 2, HG, L], F32R)
        k_stat = rig.sb("k_stat", [AUG, HG, L], F32R)
        v_next = rig.sb("v_next", [P, 2, MT, P])
        v_stat = rig.sb("v_stat", [P, MT, P])
        prob = rig.sb("prob", [P, UNITS, 2, CH])
        part = rig.sb("part", [P, HG * QT, KC])
        negmax = rig.sb("negmax", [P, HG * QT])
        negmax_part = rig.sb("negmax_part", [P, 2, HG * QT])
        rows = rig.sb("rows", [HG * QT, 2, P])
        recip = rig.sb("recip", [P, CH])
        o_sb = rig.sb("o_sb", [P, CH])
        ones = rig.sb("ones", [P, DH])
        ident = rig.sb("ident", [P, P])
        sT = rig.ps("sT", [P, 2, 2, CH])
        smax = rig.ps("smax", [P, 2, CH])
        o_ps = rig.ps("o_ps", [P, CH])
        den = rig.ps("den", [P, CH])

        consts_in = rig.sem("consts_in")
        aug_ones = rig.sem("aug_ones")
        kv_in = rig.sem("kv_in")
        q_in = [rig.sem(f"q_in{h}") for h in range(HG)]
        q_copied = rig.sem("q_copied")
        k_copied = rig.sem("k_copied")
        v_copied = rig.sem("v_copied")
        smax_ready = rig.sem("smax_ready")
        smax_free = rig.sem("smax_free")
        negmax_step = rig.sem("negmax_step")
        rows_in = rig.sem("rows_in")
        sT_ready = rig.sem("sT_ready")
        exp_done = rig.sem("exp_done")
        pv_done = rig.sem("pv_done")
        recip_ready = rig.sem("recip_ready")
        o_ready = rig.sem("o_ready")
        o_stored = rig.sem("o_stored")
        PV0 = UNITS // 2

        with nc.Block() as block:

            @block.sync
            def _(sp):
                def load_kv(bg):
                    g, b = bg % GROUPS, bg // GROUPS
                    for r, src in enumerate((0, 0, 1)):
                        for h in range(HG):
                            sp.dma_start(
                                k_mov[r * DH:(r + 1) * DH, bg % 2, h, :].bitcast(F32)
                                .rearrange("p (c t) -> p c t", c=CPB),
                                qk_scr[1, src, g, b, :, h * DH:(h + 1) * DH, :]
                                .rearrange("c p t -> p c t")).then_inc(kv_in, 16)
                    sp.dma_start(v_next[:, bg % 2, :, :],
                                 v_scr[b, :, :, bass.ds(g * P, P)].rearrange("i p d -> p i d")
                                 ).then_inc(kv_in, 16)

                def load_q(bg, ch, h):
                    g, b = bg % GROUPS, bg // GROUPS
                    for r, src in ((1, 1), (0, 0), (2, 0)):
                        sp.dma_start(q_stat[r * DH:(r + 1) * DH, h, :].bitcast(F32),
                                     qk_scr[0, src, g, b, ch, h * DH:(h + 1) * DH, :]
                                     ).then_inc(q_in[h], 16)

                def group(bg, last):
                    for ch in range(CPB):
                        s = bg * CPB + ch
                        if ch == 0 and not last:
                            sp.wait_ge(kv_in, bg * (16 * KV_DMAS) + 16 * KV_DMAS)
                            sp.wait_ge(v_copied, s * MT)
                            load_kv(bg + 1)
                        for h in range(HG):
                            if last and ch == CPB - 1:
                                break
                            sp.wait_ge(smax_ready, s * SLOT + (h + 1) * QT * KC)
                            if ch < CPB - 1:
                                load_q(bg, ch + 1, h)
                            else:
                                load_q(bg + 1, 0, h)
                        sp.wait_ge(smax_free, s * SLOT + 2 + SLOT)
                        for r in range(2):
                            sp.dma_start(
                                q_mov[ROWS + r:ROWS + r + 1, s % 2, :, :].bitcast(F32)
                                .rearrange("o h (q t) -> o (h q) t", q=QT),
                                rows[:, r, :]).then_inc(rows_in, 16)

                load_kv(0)
                for h in range(HG):
                    load_q(0, 0, h)
                sp.dma_start(ones[:, :], ones_in[:, 0:DH]).then_inc(consts_in, 16)
                sp.dma_start(ident[:, :], ident_in[:, :]).then_inc(consts_in, 16)
                with sp.Fori(0, B * GROUPS - 1) as bg:
                    group(bg, False)
                group(B * GROUPS - 1, True)

            @block.gpsimd
            def _(pool):
                def copies(s, first):
                    for h in range(HG):
                        pool.wait_ge(q_in[h], s * 48 + 48)
                        if not first:
                            pool.wait_ge(sT_ready, s * UPS - UPS)
                        pool.tensor_copy(q_mov[0:ROWS, s % 2, h, :],
                                         q_stat[:, h, :].bitcast(F32)).then_inc(q_copied, 1)
                    pool.wait_ge(kv_in, s // CPB * (16 * KV_DMAS) + 16 * KV_DMAS)
                    par = s // CPB % 2
                    for i in range(MT):
                        if not first:
                            pool.wait_ge(sT_ready, s * UPS - UPS + 2 * i + 2)
                        pool.tensor_copy(k_stat[0:ROWS, :, i * P:(i + 1) * P],
                                         k_mov[:, par, :, i * P:(i + 1) * P].bitcast(F32)
                                         ).then_inc(k_copied, 1)
                        if not first:
                            pool.wait_ge(pv_done, s * MT - MT + PV0 + i + 1)
                        pool.tensor_copy(v_stat[:, i, :], v_next[:, par, i, :]
                                         ).then_inc(v_copied, 1)

                def store_o(bg, ch):
                    pool.dma_start(o_scr[bg % GROUPS, bg // GROUPS, ch, :, :], o_sb[:, :]
                                   ).then_inc(o_stored, 16)

                copies(0, True)
                with pool.Fori(1, STAGES) as s:
                    copies(s, False)
                    pool.wait_ge(o_ready, s)
                    store_o((s - 1) // CPB, (s - 1) % CPB)
                pool.wait_ge(o_ready, STAGES)
                store_o(B * GROUPS - 1, CPB - 1)
                pool.wait_ge(o_stored, 16 * STAGES)

            @block.scalar
            def _(act):
                act.sem_inc(exp_done, 2)
                with act.Fori(0, STAGES) as s:
                    for n in range(UPS):
                        act.wait_ge(sT_ready, s * UPS + n + 1)
                        act.wait_ge(pv_done, s * MT + n // 2 + 1)
                        act.activation(prob[:, n % UNITS, :, :], sT[:, n % 2, :, :], ACT.Exp,
                                       scale=SCALE).then_inc(exp_done, 1)

            @block.vector
            def _(dve):
                dve.sem_inc(smax_free, 2)

                def maxima(s):
                    for k in range(MAXMM):
                        dve.wait_ge(smax_ready, s * SLOT + k + 1)
                        dve.tensor_reduce(part[:, k // KC, k % KC:k % KC + 1], smax[:, k % 2, :],
                                          AX_X, ALU.max).then_inc(smax_free, 1)
                    dve.wait_ge(smax_free, s * SLOT + 2 + MAXMM)
                    dve.tensor_reduce(negmax[:, :], part[:, :, :], AX_X, ALU.max, negate=True
                                      ).then_inc(negmax_step, 1)
                    dve.wait_ge(negmax_step, s * 3 + 1)
                    dve.tensor_copy(negmax_part[:, 0, :].bitcast(F32R), negmax[:, :]
                                    ).then_inc(negmax_step, 1)
                    dve.wait_ge(negmax_step, s * 3 + 2)
                    dve.tensor_tensor(negmax_part[:, 1, :], negmax[:, :],
                                      negmax_part[:, 0, :], ALU.subtract).then_inc(negmax_step, 1)
                    dve.wait_ge(rows_in, s * 32)
                    for r in range(2):
                        dve.wait_ge(smax_ready, s * SLOT + MAXMM + r + 1)
                        dve.tensor_copy(rows[:, r, :], smax[0:HG * QT, r, 0:P]
                                        ).then_inc(smax_free, 1)

                def output(s):
                    dve.wait_ge(pv_done, s * MT + PV0 + MT)
                    dve.reciprocal(recip[:, :], den[:, :]).then_inc(recip_ready, 1)
                    dve.wait_ge(recip_ready, s + 1)
                    dve.wait_ge(o_stored, s * 16)
                    dve.tensor_tensor(o_sb[:, :], o_ps[:, :], recip[:, :], ALU.mult
                                      ).then_inc(o_ready, 1)

                dve.memset(k_stat[ROWS:AUG, :, :].bitcast(F32), 1.0).then_inc(aug_ones, 1)
                maxima(0)
                with dve.Fori(1, STAGES) as s:
                    maxima(s)
                    output(s - 1)
                output(STAGES - 1)

            @block.tensor
            def _(pe):
                MAX_STEPS = 14

                def scores_T(s, i, pair):
                    n = 2 * i + pair
                    pe.wait_ge(exp_done, s * UPS + n + 1)
                    for j in range(2):
                        h = 2 * pair + j
                        mm = pe.matmul(sT[:, n % 2, j, :], k_stat[:, h, i * P:(i + 1) * P],
                                       q_mov[:, s % 2, h, :], start=True, stop=True)
                    mm.then_inc(sT_ready, 1)

                def scores_for_max(s, k):
                    h, q, kc = k // (QT * KC), k // KC % QT, k % KC
                    if k % (QT * KC) == 0:
                        pe.wait_ge(q_in[h], s * 48 + 48)
                    if k % (QT * KC) == QT * KC - 1:
                        pe.wait_ge(q_copied, s * HG + h + 1)
                    pe.wait_ge(smax_free, s * SLOT + k + 1)
                    pe.matmul(smax[:, k % 2, :], q_stat[:, h, q * P:(q + 1) * P],
                              k_mov[:, s // CPB % 2, h, kc * CH:(kc + 1) * CH],
                              start=True, stop=True).then_inc(smax_ready, 1)

                def transpose_max(s):
                    pe.wait_ge(negmax_step, s * 3 + 3)
                    for r in range(2):
                        pe.wait_ge(smax_free, s * SLOT + MAXMM + r + 1)
                        pe.transpose(smax[0:HG * QT, r, 0:P], negmax_part[:, r, :], ident[:, :]
                                     ).then_inc(smax_ready, 1)

                def times_v(s, i):
                    pe.wait_ge(exp_done, s * UPS + 2 + 2 * i + 2)
                    pe.wait_ge(v_copied, s * MT + i + 1)
                    if i == 0:
                        pe.wait_ge(o_ready, s)
                    for lhs, out in ((v_stat, o_ps), (None, den)):
                        for h in range(HG):
                            cols = slice(h * DH, (h + 1) * DH)
                            stat = ones[:, :] if lhs is None else lhs[:, i, cols]
                            mm = pe.matmul(out[cols, :], stat,
                                           prob[:, (2 * i + h // 2) % UNITS, h % 2, :],
                                           start=(i == 0), stop=(i == MT - 1))
                    mm.then_inc(pv_done, 1)

                def stage(s, with_max, with_softmax):
                    if with_max:
                        pe.wait_ge(kv_in, s // CPB * (16 * KV_DMAS) + 16 * KV_DMAS)
                    if with_softmax:
                        pe.wait_ge(rows_in, s * 32)
                        pe.wait_ge(q_copied, s * HG)
                    for i in range(MT):
                        ks = list(range(MAXMM * i // MAX_STEPS,
                                        min(MAXMM * (i + 1) // MAX_STEPS, MAXMM)))
                        for pair in range(2):
                            if with_softmax:
                                if pair == 0:
                                    pe.wait_ge(k_copied, s * MT - MT + i + 1)
                                scores_T(s - 1, i, pair)
                            if with_max:
                                half = (len(ks) + 1) // 2
                                for k in ks[:half] if pair == 0 else ks[half:]:
                                    scores_for_max(s, k)
                        if with_max and i == MAX_STEPS:
                            transpose_max(s)
                        if with_softmax and i > 0:
                            times_v(s - 1, i - 1)
                    if with_softmax:
                        times_v(s - 1, MT - 1)

                pe.sem_inc(pv_done, PV0)
                pe.wait_ge(consts_in, 32)
                pe.wait_ge(aug_ones, 1)
                stage(0, True, False)
                with pe.Fori(1, STAGES) as s:
                    stage(s, True, True)
                stage(STAGES, False, True)


def feed(nc, xT, woT, w_blocks, ones_in, o_scr, out, mod):
    HB = 2 * P
    NB = HIDDEN // HB
    HT = HB // P
    WIDTH = 2 * KT * HB + HT * D
    TPB = CPB * HT
    ITER = 2 * TPB
    with ExitStack() as ctx:
        rig = Rig(nc, ctx, "p3")
        h = rig.sb("h", [P, 2, CPB, KT, CH], F32R)
        y = rig.sb("y", [P, CPB, KT, CH])
        wo_part = rig.sb("wo_part", [P, 2, KT, D], F32R)
        w_raw = rig.sb("w_raw", [P, WIDTH])
        w_part = rig.sb("w_part", [P, 2, 2, WIDTH], F32R)
        o_raw = rig.sb("o_raw", [P, KT, CH])
        x1 = rig.sb("x1", [P, KT, CH])
        rms = rig.sb("rms", [P, CH])
        inv = rig.sb("inv", [P, CH])
        gb = rig.sb("gb", [P, 2, KT])
        ones = rig.sb("ones", [P, P])
        act_sb = rig.sb("act_sb", [P, 2, CH])
        a = rig.sb("a", [P, 2, 2, CH], F32R)
        bank = rig.ps("bank", [P, 8, CH])
        sq = w_raw[:, 0:KT * CH].rearrange("p (k t) -> p k t", k=KT)
        wo_raw = w_raw[:, 0:KT * D].rearrange("p (k n) -> p k n", k=KT)

        def gate_up(parity, part, which, kt, ht):
            at = (which * KT + kt) * HB + ht * P
            return w_part[:, parity, part, at:at + P]

        def down(parity, part, ht, f):
            at = 2 * KT * HB + ht * D + f * P
            return w_part[:, parity, part, at:at + P]

        consts_in = rig.sem("consts_in")
        wo_hi = rig.sem("wo_hi")
        wo_split = rig.sem("wo_split")
        x_in = [rig.sem(f"x_in{c}") for c in range(CPB)]
        o_in = rig.sem("o_in")
        o_hi = rig.sem("o_hi")
        o_split = rig.sem("o_split")
        proj_ready = rig.sem("proj_ready")
        x1_ready = rig.sem("x1_ready")
        y_init = rig.sem("y_init")
        sq_ready = rig.sem("sq_ready")
        ss_ready = rig.sem("ss_ready")
        rms_ready = rig.sem("rms_ready")
        norm_step = rig.sem("norm_step")
        h_hi = rig.sem("h_hi")
        h_ready = rig.sem("h_ready")
        w_in = rig.sem("w_in")
        w_hi = rig.sem("w_hi")
        w_split = rig.sem("w_split")
        gu_ready = rig.sem("gu_ready")
        silu_done = rig.sem("silu_done")
        gu_free = rig.sem("gu_free")
        a_hi = rig.sem("a_hi")
        a_ready = rig.sem("a_ready")
        down_done = rig.sem("down_done")
        y_added = rig.sem("y_added")
        y_stored = rig.sem("y_stored")

        with nc.Block() as block:

            @block.sync
            def _(sp):
                def load_o(b, ch):
                    sp.dma_start(o_raw[:, :, :], o_scr[:, b, ch, :, :]
                                 .rearrange("g p t -> p g t")).then_inc(o_in, 16)

                sp.dma_start(ones[:, :], ones_in[:, :]).then_inc(consts_in, 16)
                sp.dma_start(wo_raw, woT.rearrange("(k p) n -> p k n", p=P)
                             ).then_inc(consts_in, 16)
                with sp.Fori(0, B) as b:
                    sp.wait_ge(y_stored, b * (16 * CPB))
                    for ch in range(CPB):
                        if ch > 0:
                            sp.wait_ge(o_split, b * CPB + ch)
                        load_o(b, ch)
                        sp.dma_start(y[:, ch, :, :], xT[:, b * CPB + ch, :, :]
                                     .rearrange("k p t -> p k t")).then_inc(x_in[ch], 16)
                    with sp.Fori(0, NB) as j:
                        sp.wait_ge(ss_ready, b * CPB + CPB)
                        sp.wait_ge(w_split, b * NB + j)
                        sp.dma_start(w_raw[:, :], w_blocks[j, :, :]).then_inc(w_in, 16)
                    sp.wait_ge(y_added, b * (NB * CPB) + NB * CPB)
                    for ch in range(CPB):
                        sp.dma_start(out[:, b * CPB + ch, :, :].rearrange("k p t -> p k t"),
                                     y[:, ch, :, :]).then_inc(y_stored, 16)
                sp.wait_ge(y_stored, B * CPB * 16)

            @block.gpsimd
            def _(pool):
                with pool.Fori(0, B * NB) as w:
                    pool.wait_ge(w_in, w * 16 + 16)
                    pool.wait_ge(down_done, w * TPB)
                    pool.tensor_copy(w_part[:, w % 2, 0, :], w_raw[:, :]).then_inc(w_hi, 1)
                    pool.wait_ge(w_hi, w + 1)
                    pool.tensor_tensor(w_part[:, w % 2, 1, :], w_raw[:, :],
                                       w_part[:, w % 2, 0, :].bitcast(F32), ALU.subtract
                                       ).then_inc(w_split, 1)

            @block.scalar
            def _(act):
                def o_hi_part(b, ch):
                    act.wait_ge(o_in, (b * CPB + ch) * 16 + 16)
                    act.activation(h[:, 0, ch, :, :], o_raw[:, :, :], ACT.Copy).then_inc(o_hi, 1)

                act.wait_ge(consts_in, 32)
                act.activation(wo_part[:, 0, :, :], wo_raw, ACT.Copy).then_inc(wo_hi, 1)
                act.wait_ge(wo_split, 1)
                with act.Fori(0, B) as b:
                    act.wait_ge(down_done, b * (NB * TPB) + TPB)
                    act.wait_ge(w_split, b * NB)
                    o_hi_part(b, 0)
                    for ch in range(CPB):
                        c = b * CPB + ch
                        if ch + 1 < CPB:
                            o_hi_part(b, ch + 1)
                        act.wait_ge(x1_ready, c + 1)
                        act.wait_ge(ss_ready, c)
                        act.activation(sq, x1[:, :, :], ACT.Square).then_inc(sq_ready, 1)
                        act.wait_ge(ss_ready, c + 1)
                        act.activation(rms[:, :], bank[:, 4 * ((ch + 1) % 2), :], ACT.Sqrt,
                                       scale=1.0 / D, bias=EPS).then_inc(rms_ready, 1)
                        act.wait_ge(norm_step, c * NORM + NORM)
                        act.activation(h[:, 0, ch, :, :], x1[:, :, :], ACT.Copy).then_inc(h_hi, 1)
                    with act.Fori(0, NB // 2) as hp:
                        done = (b * (NB // 2) + hp) * ITER
                        for t in range(ITER):
                            act.wait_ge(gu_ready, done + t + 1)
                            act.wait_ge(a_ready, done + t + 1)
                            act.activation(act_sb[:, t % 2, :], bank[:, 2 * (t % 2), :], ACT.Silu
                                           ).then_inc(silu_done, 1)
                            act.wait_ge(gu_free, done + t + 3)
                            act.wait_ge(down_done, done + TPB + t - 1)
                            act.activation(a[:, t % 2, 0, :], act_sb[:, t % 2, :], ACT.Copy
                                           ).then_inc(a_hi, 1)

            @block.vector
            def _(dve):
                dve.sem_inc(gu_free, 2)
                dve.sem_inc(a_ready, 2)

                def o_lo_part(b, ch):
                    dve.wait_ge(o_hi, b * CPB + ch + 1)
                    dve.tensor_tensor(h[:, 1, ch, :, :], o_raw[:, :, :],
                                      h[:, 0, ch, :, :].bitcast(F32), ALU.subtract
                                      ).then_inc(o_split, 1)

                def add_y(done, t):
                    dve.wait_ge(down_done, done + TPB + t + 1)
                    ch = t // HT % CPB
                    dve.tensor_tensor(y[:, ch, :, :], y[:, ch, :, :], bank[:, 4:8, :], ALU.add
                                      ).then_inc(y_added, 1)

                dve.wait_ge(wo_hi, 1)
                dve.tensor_tensor(wo_part[:, 1, :, :], wo_raw, wo_part[:, 0, :, :].bitcast(F32),
                                  ALU.subtract).then_inc(wo_split, 1)
                with dve.Fori(0, B) as b:
                    o_lo_part(b, 0)
                    for ch in range(CPB):
                        c = b * CPB + ch
                        if ch + 1 < CPB:
                            o_lo_part(b, ch + 1)
                        at = 4 * ((ch + 1) % 2)
                        dve.wait_ge(proj_ready, c + 1)
                        dve.wait_ge(x_in[ch], b * 16 + 16)
                        dve.wait_ge(h_ready, c)
                        dve.tensor_tensor(x1[:, :, :], bank[:, at:at + 4, :], y[:, ch, :, :],
                                          ALU.add).then_inc(x1_ready, 1)
                        dve.wait_ge(x1_ready, c + 1)
                        dve.tensor_tensor(y[:, ch, :, :], y[:, ch, :, :], x1[:, :, :], ALU.add
                                          ).then_inc(y_init, 1)
                        done = c * NORM
                        dve.wait_ge(norm_step, done)
                        dve.tensor_scalar(gb[:, :, :], mod[:, b, 2:4, :], 1.0, None, ALU.mult
                                          ).then_inc(norm_step, 1)
                        dve.wait_ge(rms_ready, c + 1)
                        dve.reciprocal(inv[:, :], rms[:, :]).then_inc(norm_step, 1)
                        dve.wait_ge(norm_step, done + 2)
                        dve.wait_ge(y_init, c + 1)
                        dve.tensor_tensor(x1[:, :, :], x1[:, :, :],
                                          inv[:, :].unsqueeze(1).broadcast_to([P, KT, CH]),
                                          ALU.mult).then_inc(norm_step, 1)
                        dve.wait_ge(norm_step, done + 3)
                        for k in range(KT):
                            dve.tensor_scalar(x1[:, k, :], x1[:, k, :], gb[:, 0, k:k + 1],
                                              gb[:, 1, k:k + 1], ALU.mult, ALU.add
                                              ).then_inc(norm_step, 1)
                        dve.wait_ge(h_hi, c + 1)
                        dve.tensor_tensor(h[:, 1, ch, :, :], x1[:, :, :],
                                          h[:, 0, ch, :, :].bitcast(F32), ALU.subtract
                                          ).then_inc(h_ready, 1)
                    with dve.Fori(0, NB // 2) as hp:
                        done = (b * (NB // 2) + hp) * ITER
                        dve.wait_ge(y_added, (b * (NB // 2) + hp) * (ITER // HT))
                        for t in range(ITER):
                            dve.wait_ge(silu_done, done + t + 1)
                            dve.tensor_tensor(act_sb[:, t % 2, :], bank[:, 2 * (t % 2) + 1, :],
                                              act_sb[:, t % 2, :], ALU.mult).then_inc(gu_free, 1)
                            dve.wait_ge(a_hi, done + t + 1)
                            dve.tensor_tensor(a[:, t % 2, 1, :], act_sb[:, t % 2, :],
                                              a[:, t % 2, 0, :].bitcast(F32), ALU.subtract
                                              ).then_inc(a_ready, 1)
                            if t >= 2 and t % 2 == 0:
                                add_y(done, t - 1)
                        add_y(done, ITER - 1)

            @block.tensor
            def _(pe):
                pe.sem_inc(down_done, TPB)

                def project_o(b, ch):
                    c, at = b * CPB + ch, 4 * ((ch + 1) % 2)
                    pe.wait_ge(o_split, c + 1)
                    if ch == 0:
                        pe.wait_ge(y_added, b * (NB * CPB))
                    elif ch == 1:
                        pe.wait_ge(gu_free, b * (NB * TPB) + 2)
                    else:
                        pe.wait_ge(x1_ready, c - 1)
                        pe.wait_ge(rms_ready, c - 1)
                    for f in range(KT):
                        n = 0
                        for g in range(KT):
                            for stat, mov in PASSES:
                                mm = pe.matmul(bank[:, at + f, :],
                                               wo_part[:, stat, g, f * P:(f + 1) * P],
                                               h[:, mov, ch, g, :], start=(n == 0),
                                               stop=(n == 3 * KT - 1))
                                n += 1
                    mm.then_inc(proj_ready, 1)

                def tile(done, t):
                    parity, ch, ht = t // TPB, t // HT % CPB, t % HT
                    pe.wait_ge(gu_free, done + t + 1)
                    for which in range(2):
                        n = 0
                        for kt in range(KT):
                            for stat, mov in PASSES:
                                mm = pe.matmul(bank[:, 2 * (t % 2) + which, :],
                                               gate_up(parity, stat, which, kt, ht),
                                               h[:, mov, ch, kt, :], start=(n == 0),
                                               stop=(n == 3 * KT - 1))
                                n += 1
                    mm.then_inc(gu_ready, 1)

                def down_tile(done, t, added):
                    parity, ht = t // TPB, t % HT
                    pe.wait_ge(a_ready, done + t + 3)
                    if ht == 0:
                        pe.wait_ge(y_added, added + t // HT)
                    for f in range(KT):
                        for n, (stat, mov) in enumerate(PASSES):
                            mm = pe.matmul(bank[:, 4 + f, :], down(parity, stat, ht, f),
                                           a[:, t % 2, mov, :], start=(ht == 0 and n == 0),
                                           stop=(ht == HT - 1 and n == 2))
                    mm.then_inc(down_done, 1)

                pe.wait_ge(consts_in, 32)
                pe.wait_ge(wo_split, 1)
                with pe.Fori(0, B) as b:
                    project_o(b, 0)
                    for ch in range(CPB):
                        c = b * CPB + ch
                        if ch + 1 < CPB:
                            project_o(b, ch + 1)
                        pe.wait_ge(sq_ready, c + 1)
                        pe.wait_ge(x1_ready, c + 1)
                        for k in range(KT):
                            mm = pe.matmul(bank[:, 4 * ((ch + 1) % 2), :], ones[:, :], sq[:, k, :],
                                           start=(k == 0), stop=(k == KT - 1))
                        mm.then_inc(ss_ready, 1)
                    with pe.Fori(0, NB // 2) as hp:
                        pe.wait_ge(h_ready, b * CPB + CPB)
                        done = (b * (NB // 2) + hp) * ITER
                        added = (b * (NB // 2) + hp) * (ITER // HT)
                        for t in range(ITER):
                            if t % TPB == 0:
                                pe.wait_ge(w_split, b * NB + hp * 2 + t // TPB + 1)
                            tile(done, t)
                            if t > 0:
                                down_tile(done, t - 1, added)
                        down_tile(done, ITER - 1, added)


def build(nc, xT, cT, wT, modT, mod_bias, woT, w_blocks, ones_in, ident_in, out):
    qk_scr = nc.dram_tensor("qk_scr", (2, 2, GROUPS, B, CPB, P, CH), F32).ap()
    v_scr = nc.dram_tensor("v_scr", (B, L // P, P, D), F32).ap()
    o_scr = nc.dram_tensor("o_scr", (GROUPS, B, CPB, P, CH), F32).ap()
    with nc.sbuf_tensor("mod", [P, B, 4, KT], F32) as mod:
        project(nc, xT, cT, wT, modT, mod_bias, ones_in, qk_scr, v_scr, mod)
        attend(nc, qk_scr, v_scr, o_scr, ones_in, ident_in)
        feed(nc, xT, woT, w_blocks, ones_in, o_scr, out, mod)


def kernel(**inputs):
    import numpy as np
    import concourse.bacc as bacc
    from concourse import mybir as mb
    from concourse.bass_utils import run_bass_kernel_spmd as run

    def w(name):
        return np.asarray(inputs["L0_cond_" + name])

    def features_first(v):
        return v.reshape(CHUNKS, CH, KT, P).transpose(2, 0, 3, 1)

    def vector(name):
        return w(name).reshape(KT, P).T

    blocks, hb = 8, 256
    gate = w("gate_w").T.reshape(KT, P, blocks, hb).transpose(2, 1, 0, 3)
    hid = w("hid_w").T.reshape(KT, P, blocks, hb).transpose(2, 1, 0, 3)
    down = w("out_w").T.reshape(blocks, hb // P, P, D).transpose(0, 2, 1, 3)
    bias = np.stack([vector(n) for n in ("g1b", "b1b", "g2b", "b2b")], axis=1)
    arrays = {
        "xT": features_first(np.asarray(inputs["x"])),
        "cT": np.asarray(inputs["cond_256"]).T,
        "wT": np.stack([w(n).T for n in ("Wq", "Wk", "Wv")]),
        "modT": np.stack([w(n).T for n in ("g1w", "b1w", "g2w", "b2w")], axis=1),
        "mod_bias": np.stack([bias, bias], axis=1),
        "woT": w("Wo").T,
        "w_blocks": np.concatenate([v.reshape(blocks, P, -1) for v in (gate, hid, down)], axis=2),
        "ones": np.ones((P, P), np.float32),
        "ident": np.eye(P, dtype=np.float32),
    }
    nc = bacc.Bacc("TRN2", target_bir_lowering=False, num_devices=1)
    arrays = {f"in_{k}": np.ascontiguousarray(v) for k, v in arrays.items()}
    args = [nc.dram_tensor(k, v.shape, mb.dt.from_np(v.dtype), kind="ExternalInput").ap()
            for k, v in arrays.items()]
    out = nc.dram_tensor("out", (KT, CHUNKS, P, CH), F32, kind="ExternalOutput").ap()
    build(nc, *args, out)
    got = run(nc, [arrays], core_ids=[0]).results[0]["out"]
    return np.ascontiguousarray(got.transpose(1, 3, 0, 2)).reshape(B, L, D)
```

```python
from contextlib import ExitStack

import concourse.bass as bass
from concourse import mybir

F32 = mybir.dt.float32
F32R = mybir.dt.float32r
ALU = mybir.AluOpType
ACT = mybir.ActivationFunctionType
AX_X = mybir.AxisListType.X

P = 128
B, L, D, HEADS, HIDDEN = 2, 2048, 512, 16, 2048
DH = D // HEADS
TOKENS = B * L
CH = 512
CHUNKS = TOKENS // CH
CPB = L // CH
KT = D // P
HG = P // DH
GROUPS = HEADS // HG
EPS = 1e-6
SCALE = 1.0 / float(DH) ** 0.5
PASSES = ((0, 0), (0, 1), (1, 0))
NORM = 3 + KT


class Rig:

    def __init__(self, nc, ctx, tag):
        self.nc, self.ctx, self.tag = nc, ctx, tag

    def sb(self, name, shape, dt=F32):
        return self.ctx.enter_context(self.nc.sbuf_tensor(f"{self.tag}_{name}", shape, dt))

    def ps(self, name, shape, dt=F32):
        return self.ctx.enter_context(self.nc.psum_tensor(f"{self.tag}_{name}", shape, dt))

    def sem(self, name):
        return self.ctx.enter_context(self.nc.semaphore(f"{self.tag}_{name}"))


def project(nc, xT, cT, wT, modT, mod_bias, ones_in, qk_scr, v_scr, mod):
    QK = 2 * GROUPS
    TILES = QK + CH // P
    BANKS = 6
    SLOTS = 4
    VSLOTS = 2
    with ExitStack() as ctx:
        rig = Rig(nc, ctx, "p1")
        w_raw = rig.sb("w_raw", [P, 3, KT, D])
        w_part = rig.sb("w_part", [P, 2, 3, KT, D], F32R)
        mod_w = rig.sb("mod_w", [P, 4, D])
        cond = rig.sb("cond", [P, B])
        bias = rig.sb("bias", [P, B, 4, KT])
        gb = rig.sb("gb", [P, 2, KT])
        ones = rig.sb("ones", [P, P])
        xc = rig.sb("xc", [P, 2, KT, CH])
        sq = rig.sb("sq", [P, KT, CH])
        rms = rig.sb("rms", [P, CH])
        inv = rig.sb("inv", [P, CH])
        h = rig.sb("h", [P, 2, 2, KT, CH], F32R)
        out_qk = rig.sb("out_qk", [P, SLOTS, 2, CH])
        out_v = rig.sb("out_v", [P, VSLOTS, D])
        tile = rig.ps("tile", [P, BANKS, CH])
        ss = rig.ps("ss", [P, CH])
        mod_ps = rig.ps("mod_ps", [P, B, 4, KT])

        consts_in = rig.sem("consts_in")
        weights_in = rig.sem("weights_in")
        weight_hi = rig.sem("weight_hi")
        weights_split = rig.sem("weights_split")
        mod_sums = rig.sem("mod_sums")
        mod_ready = rig.sem("mod_ready")
        x_in = [rig.sem(f"x_in{i}") for i in range(2)]
        sq_ready = rig.sem("sq_ready")
        ss_ready = rig.sem("ss_ready")
        rms_ready = rig.sem("rms_ready")
        norm_step = rig.sem("norm_step")
        h_hi = rig.sem("h_hi")
        h_ready = rig.sem("h_ready")
        tile_ready = rig.sem("tile_ready")
        tile_hi = rig.sem("tile_hi")
        tile_free = rig.sem("tile_free")
        qk_stored = [rig.sem(f"qk_stored{i}") for i in range(SLOTS)]
        v_stored = [rig.sem(f"v_stored{i}") for i in range(VSLOTS)]

        with nc.Block() as block:

            @block.gpsimd
            def _(pool):
                def load_x(c, par):
                    pool.dma_start(xc[:, par, :, :], xT[:, c, :, :].rearrange("k p t -> p k t")
                                   ).then_inc(x_in[par], 16)

                load_x(0, 0)
                pool.dma_start(ones[:, :], ones_in[:, :]).then_inc(consts_in, 16)
                pool.dma_start(cond[:, :], cT[:, :]).then_inc(consts_in, 16)
                pool.dma_start(bias[:, :, :, :], mod_bias[:, :, :, :]).then_inc(consts_in, 16)
                pool.dma_start(mod_w[:, :, :], modT[:, :, :]).then_inc(consts_in, 16)
                load_x(1, 1)
                with pool.Fori(1, CHUNKS // 2) as it:
                    for par in range(2):
                        c = it * 2 + par
                        pool.wait_ge(h_ready, c - 1)
                        load_x(c, par)

            @block.sync
            def _(sp):
                for j in range(3):
                    sp.dma_start(w_raw[:, j, :, :], wT[j].rearrange("(k p) n -> p k n", p=P)
                                 ).then_inc(weights_in, 16)
                with sp.Fori(0, CHUNKS) as c:
                    for k in range(TILES):
                        sp.wait_ge(tile_free, c * TILES + BANKS + k + 1)
                        if k < QK:
                            for part in range(2):
                                sp.dma_start(qk_scr[k % 2, part, k // 2, c // CPB, c % CPB, :, :],
                                             out_qk[:, k % SLOTS, part, :]
                                             ).then_inc(qk_stored[k % SLOTS], 16)
                        else:
                            j = k - QK
                            sp.dma_start(v_scr[c // CPB, c % CPB * (CH // P) + j, :, :], out_v[:, j % VSLOTS, :]
                                         ).then_inc(v_stored[j % VSLOTS], 16)
                for s in range(SLOTS):
                    sp.wait_ge(qk_stored[s], 32 * (QK // SLOTS) * CHUNKS)
                for s in range(VSLOTS):
                    sp.wait_ge(v_stored[s], 16 * (TILES - QK) // VSLOTS * CHUNKS)

            @block.scalar
            def _(act):
                def square(c, par, x_count):
                    act.wait_ge(x_in[par], x_count)
                    act.wait_ge(ss_ready, c)
                    act.activation(sq[:, :, :], xc[:, par, :, :], ACT.Square).then_inc(sq_ready, 1)

                def root(c):
                    act.wait_ge(ss_ready, c + 1)
                    act.activation(rms[:, :], ss[:, :], ACT.Sqrt, scale=1.0 / D, bias=EPS
                                   ).then_inc(rms_ready, 1)

                def norm_hi(c, par):
                    act.wait_ge(norm_step, (c + 1) * NORM)
                    act.activation(h[:, par, 0, :, :], xc[:, par, :, :], ACT.Copy
                                   ).then_inc(h_hi, 1)

                def chunk(c, par, x_count, norm_next):
                    if norm_next:
                        square(c + 1, 1 - par, x_count)
                    for k in range(QK):
                        act.wait_ge(tile_ready, c * TILES + k + 1)
                        act.wait_ge(qk_stored[k % SLOTS],
                                    c * (32 * (QK // SLOTS)) + 32 * (k // SLOTS))
                        act.activation(out_qk[:, k % SLOTS, 0, :].bitcast(F32R),
                                       tile[:, k % BANKS, :], ACT.Copy).then_inc(tile_hi, 1)
                        if norm_next and k == 3:
                            root(c + 1)
                    if norm_next:
                        norm_hi(c + 1, 1 - par)

                act.wait_ge(x_in[0], 16)
                act.activation(sq[:, :, :], xc[:, 0, :, :], ACT.Square).then_inc(sq_ready, 1)
                act.wait_ge(weights_in, 48)
                for j in range(3):
                    act.activation(w_part[:, 0, j, :, :], w_raw[:, j, :, :], ACT.Copy
                                   ).then_inc(weight_hi, 1)
                root(0)
                norm_hi(0, 0)
                with act.Fori(0, CHUNKS // 2 - 1) as it:
                    chunk(it * 2, 0, it * 16 + 16, True)
                    chunk(it * 2 + 1, 1, it * 16 + 32, True)
                chunk(CHUNKS - 2, 0, 16 * (CHUNKS // 2), True)
                chunk(CHUNKS - 1, 1, None, False)

            @block.vector
            def _(dve):
                dve.sem_inc(tile_free, BANKS)

                def norm(c, par):
                    done = c * NORM
                    dve.wait_ge(norm_step, done)
                    dve.tensor_scalar(gb[:, :, :], mod[:, c // CPB, 0:2, :], 1.0, None, ALU.mult
                                      ).then_inc(norm_step, 1)
                    dve.wait_ge(rms_ready, c + 1)
                    dve.reciprocal(inv[:, :], rms[:, :]).then_inc(norm_step, 1)
                    dve.wait_ge(norm_step, done + 2)
                    dve.tensor_tensor(xc[:, par, :, :], xc[:, par, :, :],
                                      inv[:, :].unsqueeze(1).broadcast_to([P, KT, CH]),
                                      ALU.mult).then_inc(norm_step, 1)
                    dve.wait_ge(norm_step, done + 3)
                    for k in range(KT):
                        dve.tensor_scalar(xc[:, par, k, :], xc[:, par, k, :], gb[:, 0, k:k + 1],
                                          gb[:, 1, k:k + 1], ALU.mult, ALU.add
                                          ).then_inc(norm_step, 1)

                def norm_lo(c, par):
                    dve.wait_ge(h_hi, c + 1)
                    dve.tensor_tensor(h[:, par, 1, :, :], xc[:, par, :, :],
                                      h[:, par, 0, :, :].bitcast(F32), ALU.subtract
                                      ).then_inc(h_ready, 1)

                def chunk(c, par, norm_next):
                    for k in range(QK):
                        dve.wait_ge(tile_hi, c * QK + k + 1)
                        dve.tensor_tensor(out_qk[:, k % SLOTS, 1, :].bitcast(F32R),
                                          tile[:, k % BANKS, :], out_qk[:, k % SLOTS, 0, :],
                                          ALU.subtract).then_inc(tile_free, 1)
                        if norm_next and k == 3:
                            norm(c + 1, 1 - par)
                    if norm_next:
                        norm_lo(c + 1, 1 - par)
                    for k in range(QK, TILES):
                        j = k - QK
                        dve.wait_ge(tile_ready, c * TILES + k + 1)
                        dve.wait_ge(v_stored[j % VSLOTS],
                                    c * (16 * (TILES - QK) // VSLOTS) + 16 * (j // VSLOTS))
                        dve.tensor_copy(out_v[:, j % VSLOTS, :], tile[:, k % BANKS, :]
                                        ).then_inc(tile_free, 1)

                dve.wait_ge(mod_sums, 1)
                dve.tensor_tensor(mod[:, :, :, :], mod_ps[:, :, :, :], bias[:, :, :, :], ALU.add
                                  ).then_inc(mod_ready, 1)
                dve.wait_ge(mod_ready, 1)
                for j in range(3):
                    dve.wait_ge(weight_hi, j + 1)
                    dve.tensor_tensor(w_part[:, 1, j, :, :], w_raw[:, j, :, :],
                                      w_part[:, 0, j, :, :].bitcast(F32), ALU.subtract
                                      ).then_inc(weights_split, 1)
                norm(0, 0)
                norm_lo(0, 0)
                with dve.Fori(0, CHUNKS // 2 - 1) as it:
                    chunk(it * 2, 0, True)
                    chunk(it * 2 + 1, 1, True)
                chunk(CHUNKS - 2, 0, True)
                chunk(CHUNKS - 1, 1, False)

            @block.tensor
            def _(pe):
                def sum_squares(c):
                    pe.wait_ge(sq_ready, c + 1)
                    pe.wait_ge(rms_ready, c)
                    for k in range(KT):
                        mm = pe.matmul(ss[:, :], ones[:, :], sq[:, k, :], start=(k == 0),
                                       stop=(k == KT - 1))
                    mm.then_inc(ss_ready, 1)

                def chunk(c, par, norm_next):
                    pe.wait_ge(h_ready, c + 1)
                    for k in range(TILES):
                        pe.wait_ge(tile_free, c * TILES + k + 1)
                        n = 0
                        for kt in range(KT):
                            for stat, mov in PASSES:
                                if k < QK:
                                    g = k // 2
                                    lhs = w_part[:, stat, k % 2, kt, g * P:(g + 1) * P]
                                    rhs = h[:, par, mov, kt, :]
                                else:
                                    j = k - QK
                                    lhs = h[:, par, stat, kt, j * P:(j + 1) * P]
                                    rhs = w_part[:, mov, 2, kt, :]
                                mm = pe.matmul(tile[:, k % BANKS, :], lhs, rhs, start=(n == 0),
                                               stop=(n == 3 * KT - 1))
                                n += 1
                        mm.then_inc(tile_ready, 1)
                        if norm_next and k == 1:
                            sum_squares(c + 1)

                pe.wait_ge(consts_in, 64)
                for v in range(4):
                    for kt in range(KT):
                        mm = pe.matmul(mod_ps[:, :, v, kt], mod_w[:, v, kt * P:(kt + 1) * P],
                                       cond[:, :], start=True, stop=True)
                mm.then_inc(mod_sums, 1)
                sum_squares(0)
                pe.wait_ge(weights_split, 3)
                with pe.Fori(0, CHUNKS // 2 - 1) as it:
                    chunk(it * 2, 0, True)
                    chunk(it * 2 + 1, 1, True)
                chunk(CHUNKS - 2, 0, True)
                chunk(CHUNKS - 1, 1, False)


def attend(nc, qk_scr, v_scr, o_scr, ones_in, ident_in):
    STAGES = B * GROUPS * CPB
    MT = L // P
    QT = CH // P
    KC = L // CH
    ROWS = 3 * DH
    AUG = ROWS + 2
    MAXMM = HG * QT * KC
    PER_STEP = MAXMM // MT
    TRANS_STEP = 13
    HEAD = PER_STEP * (MT - TRANS_STEP)
    REST = MAXMM - HEAD
    TRANS = REST + PER_STEP
    SLOTS = MAXMM + 2
    SLAB = 4
    UPS = 2 * MT
    PAIRS = MT // 2 - 1
    KV_DMAS = 3 * HG + 1
    with ExitStack() as ctx:
        rig = Rig(nc, ctx, "p2")
        q_stat = rig.sb("q_stat", [ROWS, HG, CH], F32R)
        q_mov = rig.sb("q_mov", [AUG, 2, HG, CH], F32R)
        k_mov = rig.sb("k_mov", [ROWS, 2, HG, L], F32R)
        k_stat = rig.sb("k_stat", [AUG, HG, L], F32R)
        v_next = rig.sb("v_next", [P, 2, MT, P])
        v_stat = rig.sb("v_stat", [P, MT, P])
        prob = rig.sb("prob", [P, SLAB, HG, CH])
        pair_sum = rig.sb("pair_sum", [P, 2, HG, CH])
        part = rig.sb("part", [P, HG * QT, KC])
        negmax = rig.sb("negmax", [P, HG * QT])
        negmax_part = rig.sb("negmax_part", [P, 2, HG * QT])
        rows = rig.sb("rows", [HG * QT, 2, P])
        o_sb = rig.sb("o_sb", [P, CH])
        den_sb = rig.sb("den_sb", [P, CH])
        ones = rig.sb("ones", [P, DH])
        ident = rig.sb("ident", [P, P])
        sT = rig.ps("sT", [P, 2, 2, CH])
        smax = rig.ps("smax", [P, 2, CH])
        o_ps = rig.ps("o_ps", [P, CH])
        den = rig.ps("den", [P, CH])

        consts_in = rig.sem("consts_in")
        aug_ones = rig.sem("aug_ones")
        kv_in = rig.sem("kv_in")
        kv_tile = [rig.sem(f"kv_tile{i}") for i in range(MT)]
        q_in = [rig.sem(f"q_in{h}") for h in range(HG)]
        q_copied = rig.sem("q_copied")
        smax_ready = rig.sem("smax_ready")
        smax_free = rig.sem("smax_free")
        negmax_step = rig.sem("negmax_step")
        rows_in = rig.sem("rows_in")
        sT_ready = rig.sem("sT_ready")
        exp_done = rig.sem("exp_done")
        pv_done = rig.sem("pv_done")
        pair_added = rig.sem("pair_added")
        pair_used = rig.sem("pair_used")
        evacuated = rig.sem("evacuated")
        inverse = rig.sem("inverse")
        o_ready = rig.sem("o_ready")
        o_stored = rig.sem("o_stored")

        def slot(s, x):
            return s * SLOTS + (HEAD + x)

        with nc.Block() as block:

            @block.sync
            def _(sp):
                def load_kv(bg):
                    g, b = bg % GROUPS, bg // GROUPS
                    for r, src in enumerate((0, 0, 1)):
                        for h in range(HG):
                            sp.dma_start(
                                k_mov[r * DH:(r + 1) * DH, bg % 2, h, :].bitcast(F32)
                                .rearrange("p (c t) -> p c t", c=CPB),
                                qk_scr[1, src, g, b, :, h * DH:(h + 1) * DH, :]
                                .rearrange("c p t -> p c t")).then_inc(kv_in, 16)
                    sp.dma_start(v_next[:, bg % 2, :, :],
                                 v_scr[b, :, :, bass.ds(g * P, P)].rearrange("i p d -> p i d")
                                 ).then_inc(kv_in, 16)

                def load_q(bg, ch, h):
                    g, b = bg % GROUPS, bg // GROUPS
                    for r, src in ((1, 1), (0, 0), (2, 0)):
                        sp.dma_start(q_stat[r * DH:(r + 1) * DH, h, :].bitcast(F32),
                                     qk_scr[0, src, g, b, ch, h * DH:(h + 1) * DH, :]
                                     ).then_inc(q_in[h], 16)

                def next_q(bg, ch, h):
                    sp.wait_ge(smax_ready, slot(bg * CPB + ch, (h + 1) * QT * KC - HEAD))
                    if ch < CPB - 1:
                        load_q(bg, ch + 1, h)
                    else:
                        load_q(bg + 1, 0, h)

                def send_rows(s, x):
                    sp.wait_ge(smax_free, slot(s, x) + 4)
                    for r in range(2):
                        sp.dma_start(
                            q_mov[ROWS + r:ROWS + r + 1, s % 2, :, :].bitcast(F32)
                            .rearrange("o h (q t) -> o (h q) t", q=QT),
                            rows[:, r, :]).then_inc(rows_in, 16)

                def copy_tile(bg, i):
                    sp.wait_ge(pv_done, bg * (CPB * MT) + i + 1)
                    sp.dma_start(k_stat[0:ROWS, :, i * P:(i + 1) * P].bitcast(F32),
                                 k_mov[:, bg % 2, :, i * P:(i + 1) * P].bitcast(F32)
                                 ).then_inc(kv_tile[i], 16)
                    sp.dma_start(v_stat[:, i, :], v_next[:, bg % 2, i, :]).then_inc(kv_tile[i], 16)

                def group(bg, last):
                    for ch in range(CPB):
                        s = bg * CPB + ch
                        final = last and ch == CPB - 1
                        if ch == 0:
                            sp.wait_ge(kv_in, bg * (16 * KV_DMAS) + 16 * KV_DMAS)
                        if ch == 1 and not last:
                            load_kv(bg + 1)
                        for i in range(MT):
                            if i % QT == 0 and not final:
                                next_q(bg, ch, i // QT)
                            if i == TRANS_STEP:
                                send_rows(s, REST if final else TRANS)
                            if ch == 0:
                                copy_tile(bg, i)

                load_kv(0)
                for h in range(HG):
                    load_q(0, 0, h)
                sp.dma_start(ones[:, :], ones_in[:, 0:DH]).then_inc(consts_in, 16)
                sp.dma_start(ident[:, :], ident_in[:, :]).then_inc(consts_in, 16)
                with sp.Fori(0, B * GROUPS - 1) as bg:
                    group(bg, False)
                group(B * GROUPS - 1, True)

            @block.gpsimd
            def _(pool):
                def copy_q(s, used):
                    for h in range(HG):
                        pool.wait_ge(q_in[h], s * 48 + 48)
                        if used and h == 0:
                            pool.wait_ge(sT_ready, s * UPS - UPS)
                        pool.tensor_copy(q_mov[0:ROWS, s % 2, h, :],
                                         q_stat[:, h, :].bitcast(F32)).then_inc(q_copied, 1)

                def add_pairs(c, store_last):
                    for j in range(PAIRS):
                        pool.wait_ge(exp_done, c * UPS + 4 * j + 6)
                        pool.wait_ge(pair_used, c * PAIRS + (j + 1 if j > 1 else 2 - j))
                        at = 2 * j % SLAB
                        pool.tensor_tensor(pair_sum[:, j % 2, :, :], prob[:, at, :, :],
                                           prob[:, at + 1, :, :], ALU.add
                                           ).then_inc(pair_added, 1)
                        if j == PAIRS - 2 and store_last:
                            store_o(c - 1)

                def store_o(c):
                    pool.wait_ge(o_ready, c + 1)
                    pool.dma_start(o_scr[c // CPB % GROUPS, c // CPB // GROUPS, c % CPB, :, :],
                                   o_sb[:, :]).then_inc(o_stored, 16)

                pool.sem_inc(pair_added, 1)
                copy_q(0, False)
                copy_q(1, False)
                add_pairs(0, False)
                with pool.Fori(1, STAGES - 1) as c:
                    copy_q(c + 1, True)
                    add_pairs(c, True)
                add_pairs(STAGES - 1, True)
                store_o(STAGES - 1)
                pool.wait_ge(o_stored, 16 * STAGES)

            @block.scalar
            def _(act):
                act.sem_inc(exp_done, 2)
                act.sem_inc(evacuated, 2)

                def chunk(c, first):
                    for n in range(UPS):
                        i = n // 2
                        act.wait_ge(sT_ready, c * UPS + n + 1)
                        if n % 2 == 0:
                            act.wait_ge(pv_done, c * MT + (MT - SLAB) + i + 1)
                            if i >= SLAB:
                                act.wait_ge(pair_added, c * PAIRS + (i - SLAB) // 2 + 2)
                            elif i < 2:
                                act.wait_ge(pair_added, c * PAIRS + 1)
                        act.activation(prob[:, i % SLAB, n % 2 * 2:n % 2 * 2 + 2, :],
                                       sT[:, n % 2, :, :], ACT.Exp, scale=SCALE
                                       ).then_inc(exp_done, 1)
                    if not first:
                        act.wait_ge(o_stored, c * 16)
                    act.wait_ge(pv_done, c * MT + 2 * MT)
                    act.activation(den_sb[:, :], den[:, :], ACT.Copy).then_inc(evacuated, 1)
                    act.activation(o_sb[:, :], o_ps[:, :], ACT.Copy).then_inc(evacuated, 1)

                chunk(0, True)
                with act.Fori(1, STAGES) as c:
                    chunk(c, False)

            @block.vector
            def _(dve):
                OUT_AT = 8

                def reduce(at, k, x):
                    dve.wait_ge(smax_ready, at + 1)
                    dve.tensor_reduce(part[:, k // KC, k % KC:k % KC + 1], smax[:, x % 2, :],
                                      AX_X, ALU.max).then_inc(smax_free, 1)

                def output_step(c, n):
                    if n < QT:
                        if n == 0:
                            dve.wait_ge(evacuated, c * 2 + 4)
                        cols = slice(n * P, (n + 1) * P)
                        dve.reciprocal(den_sb[:, cols], den_sb[:, cols]).then_inc(inverse, 1)
                    else:
                        dve.wait_ge(inverse, c * QT + QT)
                        dve.tensor_tensor(o_sb[:, :], o_sb[:, :], den_sb[:, :], ALU.mult
                                          ).then_inc(o_ready, 1)

                def maxima(s, first, with_next, out_chunk):
                    for x in range(REST):
                        if out_chunk is not None and x >= OUT_AT and x % 4 == 0 \
                                and x < OUT_AT + 4 * (QT + 1):
                            output_step(out_chunk, (x - OUT_AT) // 4)
                        reduce(slot(s, x), HEAD + x, x)
                    dve.wait_ge(smax_free, slot(s, REST) + 2)
                    dve.tensor_reduce(negmax[:, :], part[:, :, :], AX_X, ALU.max, negate=True
                                      ).then_inc(negmax_step, 1)
                    dve.wait_ge(negmax_step, s * 3 + 1)
                    dve.tensor_copy(negmax_part[:, 0, :].bitcast(F32R), negmax[:, :]
                                    ).then_inc(negmax_step, 1)
                    dve.wait_ge(negmax_step, s * 3 + 2)
                    dve.tensor_tensor(negmax_part[:, 1, :], negmax[:, :],
                                      negmax_part[:, 0, :], ALU.subtract).then_inc(negmax_step, 1)
                    trans = TRANS if with_next else REST
                    if with_next:
                        for k in range(PER_STEP):
                            reduce(slot(s, REST + k), k, k)
                    if not first:
                        dve.wait_ge(rows_in, s * 32)
                    for r in range(2):
                        dve.wait_ge(smax_ready, slot(s, trans) + r + 1)
                        dve.tensor_copy(rows[:, r, :], smax[0:HG * QT, r, 0:P]
                                        ).then_inc(smax_free, 1)
                    if with_next:
                        for k in range(PER_STEP, HEAD):
                            reduce(slot(s, REST + 2 + k), k, k)

                dve.sem_inc(smax_free, 2)
                dve.memset(k_stat[ROWS:AUG, :, :].bitcast(F32), 1.0).then_inc(aug_ones, 1)
                for k in range(HEAD):
                    reduce(k, k, k)
                maxima(0, True, True, None)
                maxima(1, False, True, None)
                with dve.Fori(2, STAGES - 1) as s:
                    maxima(s, False, True, s - 2)
                maxima(STAGES - 1, False, False, STAGES - 3)
                for c in (STAGES - 2, STAGES - 1):
                    for n in range(QT + 1):
                        output_step(c, n)

            @block.tensor
            def _(pe):
                def scores_T(c, i, pair):
                    n = 2 * i + pair
                    pe.wait_ge(exp_done, c * UPS + n + 1)
                    for j in range(2):
                        h = 2 * pair + j
                        mm = pe.matmul(sT[:, pair, j, :], k_stat[:, h, i * P:(i + 1) * P],
                                       q_mov[:, c % 2, h, :], start=True, stop=True)
                    mm.then_inc(sT_ready, 1)

                def scores_for_max(s, k, at, bank):
                    h, q, kc = k // (QT * KC), k // KC % QT, k % KC
                    if k % (QT * KC) == 0:
                        pe.wait_ge(q_in[h], s * 48 + 48)
                    if k % (QT * KC) == QT * KC - 1:
                        pe.wait_ge(q_copied, s * HG + h + 1)
                    pe.wait_ge(smax_free, at + 1)
                    pe.matmul(smax[:, bank, :], q_stat[:, h, q * P:(q + 1) * P],
                              k_mov[:, s // CPB % 2, h, kc * CH:(kc + 1) * CH],
                              start=True, stop=True).then_inc(smax_ready, 1)

                def transpose_max(s, x):
                    pe.wait_ge(negmax_step, s * 3 + 3)
                    for r in range(2):
                        pe.wait_ge(smax_free, slot(s, x) + r + 1)
                        pe.transpose(smax[0:HG * QT, r, 0:P], negmax_part[:, r, :], ident[:, :]
                                     ).then_inc(smax_ready, 1)

                def columns(out, stat, mov, start, stop):
                    for h in range(HG):
                        cols = slice(h * DH, (h + 1) * DH)
                        mm = pe.matmul(out[cols, :], stat(cols), mov[:, h, :], start=start,
                                       stop=stop)
                    return mm

                def times_v(c, i):
                    pe.wait_ge(exp_done, c * UPS + 2 + 2 * i + 2)
                    if i == 0:
                        pe.wait_ge(evacuated, c * 2 + 2)
                    mm = columns(o_ps, lambda cols: v_stat[:, i, cols], prob[:, i % SLAB, :, :],
                                 i == 0, i == MT - 1)
                    if i < 2 * PAIRS:
                        mm.then_inc(pv_done, 1)

                def denominator_tile(i):
                    columns(den, lambda cols: ones[:, :], prob[:, i % SLAB, :, :], False,
                            i == MT - 1).then_inc(pv_done, 1)

                def denominator_pair(c, j):
                    pe.wait_ge(pair_added, c * PAIRS + j + 2)
                    columns(den, lambda cols: ones[:, :], pair_sum[:, j % 2, :, :], j == 0, False
                            ).then_inc(pair_used, 1)

                def body(s, with_max, with_softmax, with_next):
                    if with_softmax:
                        c = s - 1
                        pe.wait_ge(rows_in, c * 32 + 32)
                        pe.wait_ge(q_copied, c * HG + HG)
                    for i in range(MT):
                        def for_max(n):
                            x = PER_STEP * i + n
                            if with_max and i < TRANS_STEP:
                                scores_for_max(s, HEAD + x, slot(s, x), n % 2)
                            elif with_next:
                                if i == TRANS_STEP and n == 0:
                                    pe.wait_ge(kv_in, (s + 1) // CPB * (16 * KV_DMAS)
                                               + 16 * KV_DMAS)
                                at = x if i == TRANS_STEP else x + 2
                                scores_for_max(s + 1, x - REST, slot(s, at), n % 2)
                        if with_softmax:
                            pe.wait_ge(kv_tile[i], (s + (CPB - 1)) // CPB * 32)
                            scores_T(c, i, 0)
                        for_max(0)
                        if with_softmax:
                            scores_T(c, i, 1)
                        for_max(1)
                        if with_softmax and i > 0:
                            times_v(c, i - 1)
                        for_max(2)
                        if with_softmax and i % 2 == 0 and i >= 4:
                            denominator_pair(c, i // 2 - 2)
                        elif with_softmax and i == MT - 1:
                            denominator_tile(i - 1)
                        for_max(3)
                        if with_max and i == TRANS_STEP:
                            transpose_max(s, TRANS if with_next else REST)
                    if with_softmax:
                        denominator_pair(c, PAIRS - 1)
                        times_v(c, MT - 1)
                        denominator_tile(MT - 1)

                pe.sem_inc(pv_done, MT)
                pe.sem_inc(pair_used, 2)
                pe.wait_ge(consts_in, 32)
                pe.wait_ge(aug_ones, 1)
                pe.wait_ge(kv_in, 16 * KV_DMAS)
                for k in range(HEAD):
                    scores_for_max(0, k, k, k % 2)
                body(0, True, False, True)
                with pe.Fori(1, STAGES - 1) as s:
                    body(s, True, True, True)
                body(STAGES - 1, True, True, False)
                body(STAGES, False, True, False)


def feed(nc, xT, woT, w_blocks, ones_in, o_scr, out, mod):
    HB = 2 * P
    NB = HIDDEN // HB
    HT = HB // P
    WIDTH = 2 * KT * HB + HT * D
    TPB = CPB * HT
    ITER = 2 * TPB
    with ExitStack() as ctx:
        rig = Rig(nc, ctx, "p3")
        h = rig.sb("h", [P, 2, CPB, KT, CH], F32R)
        y = rig.sb("y", [P, CPB, KT, CH])
        wo_part = rig.sb("wo_part", [P, 2, KT, D], F32R)
        w_raw = rig.sb("w_raw", [P, WIDTH])
        w_part = rig.sb("w_part", [P, 2, 2, WIDTH], F32R)
        o_raw = rig.sb("o_raw", [P, KT, CH])
        x1 = rig.sb("x1", [P, KT, CH])
        rms = rig.sb("rms", [P, CH])
        inv = rig.sb("inv", [P, CH])
        gb = rig.sb("gb", [P, 2, KT])
        ones = rig.sb("ones", [P, P])
        act_sb = rig.sb("act_sb", [P, 2, CH])
        a = rig.sb("a", [P, 2, 2, CH], F32R)
        bank = rig.ps("bank", [P, 8, CH])
        sq = w_raw[:, 0:KT * CH].rearrange("p (k t) -> p k t", k=KT)
        wo_raw = w_raw[:, 0:KT * D].rearrange("p (k n) -> p k n", k=KT)

        def gate_up(parity, part, which, kt, ht):
            at = (which * KT + kt) * HB + ht * P
            return w_part[:, parity, part, at:at + P]

        def down(parity, part, ht, f):
            at = 2 * KT * HB + ht * D + f * P
            return w_part[:, parity, part, at:at + P]

        consts_in = rig.sem("consts_in")
        wo_hi = rig.sem("wo_hi")
        wo_split = rig.sem("wo_split")
        x_in = [rig.sem(f"x_in{c}") for c in range(CPB)]
        o_in = rig.sem("o_in")
        o_hi = rig.sem("o_hi")
        o_split = rig.sem("o_split")
        proj_ready = rig.sem("proj_ready")
        x1_ready = rig.sem("x1_ready")
        y_init = rig.sem("y_init")
        sq_ready = rig.sem("sq_ready")
        ss_ready = rig.sem("ss_ready")
        rms_ready = rig.sem("rms_ready")
        norm_step = rig.sem("norm_step")
        h_hi = rig.sem("h_hi")
        h_ready = rig.sem("h_ready")
        w_in = rig.sem("w_in")
        w_hi = rig.sem("w_hi")
        w_split = rig.sem("w_split")
        gu_ready = rig.sem("gu_ready")
        silu_done = rig.sem("silu_done")
        gu_free = rig.sem("gu_free")
        a_hi = rig.sem("a_hi")
        a_ready = rig.sem("a_ready")
        down_done = rig.sem("down_done")
        y_added = rig.sem("y_added")
        y_stored = rig.sem("y_stored")

        with nc.Block() as block:

            @block.sync
            def _(sp):
                def load_o(b, ch):
                    sp.dma_start(o_raw[:, :, :], o_scr[:, b, ch, :, :]
                                 .rearrange("g p t -> p g t")).then_inc(o_in, 16)

                sp.dma_start(ones[:, :], ones_in[:, :]).then_inc(consts_in, 16)
                sp.dma_start(wo_raw, woT.rearrange("(k p) n -> p k n", p=P)
                             ).then_inc(consts_in, 16)
                with sp.Fori(0, B) as b:
                    sp.wait_ge(y_stored, b * (16 * CPB))
                    for ch in range(CPB):
                        if ch > 0:
                            sp.wait_ge(o_split, b * CPB + ch)
                        load_o(b, ch)
                        sp.dma_start(y[:, ch, :, :], xT[:, b * CPB + ch, :, :]
                                     .rearrange("k p t -> p k t")).then_inc(x_in[ch], 16)
                    with sp.Fori(0, NB) as j:
                        sp.wait_ge(ss_ready, b * CPB + CPB)
                        sp.wait_ge(w_split, b * NB + j)
                        sp.dma_start(w_raw[:, :], w_blocks[j, :, :]).then_inc(w_in, 16)
                    sp.wait_ge(y_added, b * (NB * CPB) + NB * CPB)
                    for ch in range(CPB):
                        sp.dma_start(out[:, b * CPB + ch, :, :].rearrange("k p t -> p k t"),
                                     y[:, ch, :, :]).then_inc(y_stored, 16)
                sp.wait_ge(y_stored, B * CPB * 16)

            @block.gpsimd
            def _(pool):
                with pool.Fori(0, B * NB) as w:
                    pool.wait_ge(w_in, w * 16 + 16)
                    pool.wait_ge(down_done, w * TPB)
                    pool.tensor_copy(w_part[:, w % 2, 0, :], w_raw[:, :]).then_inc(w_hi, 1)
                    pool.wait_ge(w_hi, w + 1)
                    pool.tensor_tensor(w_part[:, w % 2, 1, :], w_raw[:, :],
                                       w_part[:, w % 2, 0, :].bitcast(F32), ALU.subtract
                                       ).then_inc(w_split, 1)

            @block.scalar
            def _(act):
                def o_hi_part(b, ch):
                    act.wait_ge(o_in, (b * CPB + ch) * 16 + 16)
                    act.activation(h[:, 0, ch, :, :], o_raw[:, :, :], ACT.Copy).then_inc(o_hi, 1)

                act.wait_ge(consts_in, 32)
                act.activation(wo_part[:, 0, :, :], wo_raw, ACT.Copy).then_inc(wo_hi, 1)
                act.wait_ge(wo_split, 1)
                with act.Fori(0, B) as b:
                    act.wait_ge(down_done, b * (NB * TPB) + TPB)
                    act.wait_ge(w_split, b * NB)
                    o_hi_part(b, 0)
                    for ch in range(CPB):
                        c = b * CPB + ch
                        if ch + 1 < CPB:
                            o_hi_part(b, ch + 1)
                        act.wait_ge(x1_ready, c + 1)
                        act.wait_ge(ss_ready, c)
                        act.activation(sq, x1[:, :, :], ACT.Square).then_inc(sq_ready, 1)
                        act.wait_ge(ss_ready, c + 1)
                        act.activation(rms[:, :], bank[:, 4 * ((ch + 1) % 2), :], ACT.Sqrt,
                                       scale=1.0 / D, bias=EPS).then_inc(rms_ready, 1)
                        act.wait_ge(norm_step, c * NORM + NORM)
                        act.activation(h[:, 0, ch, :, :], x1[:, :, :], ACT.Copy).then_inc(h_hi, 1)
                    with act.Fori(0, NB // 2) as hp:
                        done = (b * (NB // 2) + hp) * ITER
                        for t in range(ITER):
                            act.wait_ge(gu_ready, done + t + 1)
                            act.wait_ge(a_ready, done + t + 1)
                            act.activation(act_sb[:, t % 2, :], bank[:, 2 * (t % 2), :], ACT.Silu
                                           ).then_inc(silu_done, 1)
                            act.wait_ge(gu_free, done + t + 3)
                            act.wait_ge(down_done, done + TPB + t - 1)
                            act.activation(a[:, t % 2, 0, :], act_sb[:, t % 2, :], ACT.Copy
                                           ).then_inc(a_hi, 1)

            @block.vector
            def _(dve):
                dve.sem_inc(gu_free, 2)
                dve.sem_inc(a_ready, 2)

                def o_lo_part(b, ch):
                    dve.wait_ge(o_hi, b * CPB + ch + 1)
                    dve.tensor_tensor(h[:, 1, ch, :, :], o_raw[:, :, :],
                                      h[:, 0, ch, :, :].bitcast(F32), ALU.subtract
                                      ).then_inc(o_split, 1)

                def add_y(done, t):
                    dve.wait_ge(down_done, done + TPB + t + 1)
                    ch = t // HT % CPB
                    dve.tensor_tensor(y[:, ch, :, :], y[:, ch, :, :], bank[:, 4:8, :], ALU.add
                                      ).then_inc(y_added, 1)

                dve.wait_ge(wo_hi, 1)
                dve.tensor_tensor(wo_part[:, 1, :, :], wo_raw, wo_part[:, 0, :, :].bitcast(F32),
                                  ALU.subtract).then_inc(wo_split, 1)
                with dve.Fori(0, B) as b:
                    o_lo_part(b, 0)
                    for ch in range(CPB):
                        c = b * CPB + ch
                        if ch + 1 < CPB:
                            o_lo_part(b, ch + 1)
                        at = 4 * ((ch + 1) % 2)
                        dve.wait_ge(proj_ready, c + 1)
                        dve.wait_ge(x_in[ch], b * 16 + 16)
                        dve.wait_ge(h_ready, c)
                        dve.tensor_tensor(x1[:, :, :], bank[:, at:at + 4, :], y[:, ch, :, :],
                                          ALU.add).then_inc(x1_ready, 1)
                        dve.wait_ge(x1_ready, c + 1)
                        dve.tensor_tensor(y[:, ch, :, :], y[:, ch, :, :], x1[:, :, :], ALU.add
                                          ).then_inc(y_init, 1)
                        done = c * NORM
                        dve.wait_ge(norm_step, done)
                        dve.tensor_scalar(gb[:, :, :], mod[:, b, 2:4, :], 1.0, None, ALU.mult
                                          ).then_inc(norm_step, 1)
                        dve.wait_ge(rms_ready, c + 1)
                        dve.reciprocal(inv[:, :], rms[:, :]).then_inc(norm_step, 1)
                        dve.wait_ge(norm_step, done + 2)
                        dve.wait_ge(y_init, c + 1)
                        dve.tensor_tensor(x1[:, :, :], x1[:, :, :],
                                          inv[:, :].unsqueeze(1).broadcast_to([P, KT, CH]),
                                          ALU.mult).then_inc(norm_step, 1)
                        dve.wait_ge(norm_step, done + 3)
                        for k in range(KT):
                            dve.tensor_scalar(x1[:, k, :], x1[:, k, :], gb[:, 0, k:k + 1],
                                              gb[:, 1, k:k + 1], ALU.mult, ALU.add
                                              ).then_inc(norm_step, 1)
                        dve.wait_ge(h_hi, c + 1)
                        dve.tensor_tensor(h[:, 1, ch, :, :], x1[:, :, :],
                                          h[:, 0, ch, :, :].bitcast(F32), ALU.subtract
                                          ).then_inc(h_ready, 1)
                    with dve.Fori(0, NB // 2) as hp:
                        done = (b * (NB // 2) + hp) * ITER
                        dve.wait_ge(y_added, (b * (NB // 2) + hp) * (ITER // HT))
                        for t in range(ITER):
                            dve.wait_ge(silu_done, done + t + 1)
                            dve.tensor_tensor(act_sb[:, t % 2, :], bank[:, 2 * (t % 2) + 1, :],
                                              act_sb[:, t % 2, :], ALU.mult).then_inc(gu_free, 1)
                            dve.wait_ge(a_hi, done + t + 1)
                            dve.tensor_tensor(a[:, t % 2, 1, :], act_sb[:, t % 2, :],
                                              a[:, t % 2, 0, :].bitcast(F32), ALU.subtract
                                              ).then_inc(a_ready, 1)
                            if t >= 2 and t % 2 == 0:
                                add_y(done, t - 1)
                        add_y(done, ITER - 1)

            @block.tensor
            def _(pe):
                pe.sem_inc(down_done, TPB)

                def project_o(b, ch):
                    c, at = b * CPB + ch, 4 * ((ch + 1) % 2)
                    pe.wait_ge(o_split, c + 1)
                    if ch == 0:
                        pe.wait_ge(y_added, b * (NB * CPB))
                    elif ch == 1:
                        pe.wait_ge(gu_free, b * (NB * TPB) + 2)
                    else:
                        pe.wait_ge(x1_ready, c - 1)
                        pe.wait_ge(rms_ready, c - 1)
                    for f in range(KT):
                        n = 0
                        for g in range(KT):
                            for stat, mov in PASSES:
                                mm = pe.matmul(bank[:, at + f, :],
                                               wo_part[:, stat, g, f * P:(f + 1) * P],
                                               h[:, mov, ch, g, :], start=(n == 0),
                                               stop=(n == 3 * KT - 1))
                                n += 1
                    mm.then_inc(proj_ready, 1)

                def tile(done, t):
                    parity, ch, ht = t // TPB, t // HT % CPB, t % HT
                    pe.wait_ge(gu_free, done + t + 1)
                    for which in range(2):
                        n = 0
                        for kt in range(KT):
                            for stat, mov in PASSES:
                                mm = pe.matmul(bank[:, 2 * (t % 2) + which, :],
                                               gate_up(parity, stat, which, kt, ht),
                                               h[:, mov, ch, kt, :], start=(n == 0),
                                               stop=(n == 3 * KT - 1))
                                n += 1
                    mm.then_inc(gu_ready, 1)

                def down_tile(done, t, added):
                    parity, ht = t // TPB, t % HT
                    pe.wait_ge(a_ready, done + t + 3)
                    if ht == 0:
                        pe.wait_ge(y_added, added + t // HT)
                    for f in range(KT):
                        for n, (stat, mov) in enumerate(PASSES):
                            mm = pe.matmul(bank[:, 4 + f, :], down(parity, stat, ht, f),
                                           a[:, t % 2, mov, :], start=(ht == 0 and n == 0),
                                           stop=(ht == HT - 1 and n == 2))
                    mm.then_inc(down_done, 1)

                pe.wait_ge(consts_in, 32)
                pe.wait_ge(wo_split, 1)
                with pe.Fori(0, B) as b:
                    project_o(b, 0)
                    for ch in range(CPB):
                        c = b * CPB + ch
                        if ch + 1 < CPB:
                            project_o(b, ch + 1)
                        pe.wait_ge(sq_ready, c + 1)
                        pe.wait_ge(x1_ready, c + 1)
                        for k in range(KT):
                            mm = pe.matmul(bank[:, 4 * ((ch + 1) % 2), :], ones[:, :], sq[:, k, :],
                                           start=(k == 0), stop=(k == KT - 1))
                        mm.then_inc(ss_ready, 1)
                    with pe.Fori(0, NB // 2) as hp:
                        pe.wait_ge(h_ready, b * CPB + CPB)
                        done = (b * (NB // 2) + hp) * ITER
                        added = (b * (NB // 2) + hp) * (ITER // HT)
                        for t in range(ITER):
                            if t % TPB == 0:
                                pe.wait_ge(w_split, b * NB + hp * 2 + t // TPB + 1)
                            tile(done, t)
                            if t > 0:
                                down_tile(done, t - 1, added)
                        down_tile(done, ITER - 1, added)


def build(nc, xT, cT, wT, modT, mod_bias, woT, w_blocks, ones_in, ident_in, out):
    qk_scr = nc.dram_tensor("qk_scr", (2, 2, GROUPS, B, CPB, P, CH), F32).ap()
    v_scr = nc.dram_tensor("v_scr", (B, L // P, P, D), F32).ap()
    o_scr = nc.dram_tensor("o_scr", (GROUPS, B, CPB, P, CH), F32).ap()
    with nc.sbuf_tensor("mod", [P, B, 4, KT], F32) as mod:
        project(nc, xT, cT, wT, modT, mod_bias, ones_in, qk_scr, v_scr, mod)
        attend(nc, qk_scr, v_scr, o_scr, ones_in, ident_in)
        feed(nc, xT, woT, w_blocks, ones_in, o_scr, out, mod)


def kernel(**inputs):
    import numpy as np
    import concourse.bacc as bacc
    from concourse import mybir as mb
    from concourse.bass_utils import run_bass_kernel_spmd as run

    def w(name):
        return np.asarray(inputs["L0_cond_" + name])

    def features_first(v):
        return v.reshape(CHUNKS, CH, KT, P).transpose(2, 0, 3, 1)

    def vector(name):
        return w(name).reshape(KT, P).T

    blocks, hb = 8, 256
    gate = w("gate_w").T.reshape(KT, P, blocks, hb).transpose(2, 1, 0, 3)
    hid = w("hid_w").T.reshape(KT, P, blocks, hb).transpose(2, 1, 0, 3)
    down = w("out_w").T.reshape(blocks, hb // P, P, D).transpose(0, 2, 1, 3)
    bias = np.stack([vector(n) for n in ("g1b", "b1b", "g2b", "b2b")], axis=1)
    arrays = {
        "xT": features_first(np.asarray(inputs["x"])),
        "cT": np.asarray(inputs["cond_256"]).T,
        "wT": np.stack([w(n).T for n in ("Wq", "Wk", "Wv")]),
        "modT": np.stack([w(n).T for n in ("g1w", "b1w", "g2w", "b2w")], axis=1),
        "mod_bias": np.stack([bias, bias], axis=1),
        "woT": w("Wo").T,
        "w_blocks": np.concatenate([v.reshape(blocks, P, -1) for v in (gate, hid, down)], axis=2),
        "ones": np.ones((P, P), np.float32),
        "ident": np.eye(P, dtype=np.float32),
    }
    nc = bacc.Bacc("TRN2", target_bir_lowering=False, num_devices=1)
    arrays = {f"in_{k}": np.ascontiguousarray(v) for k, v in arrays.items()}
    args = [nc.dram_tensor(k, v.shape, mb.dt.from_np(v.dtype), kind="ExternalInput").ap()
            for k, v in arrays.items()]
    out = nc.dram_tensor("out", (KT, CHUNKS, P, CH), F32, kind="ExternalOutput").ap()
    build(nc, *args, out)
    got = run(nc, [arrays], core_ids=[0]).results[0]["out"]
    return np.ascontiguousarray(got.transpose(1, 3, 0, 2)).reshape(B, L, D)
```

```python
from contextlib import ExitStack

import concourse.bass as bass
from concourse import mybir

F32 = mybir.dt.float32
F32R = mybir.dt.float32r
ALU = mybir.AluOpType
ACT = mybir.ActivationFunctionType
AX_X = mybir.AxisListType.X

P = 128
B, L, D, HEADS, HIDDEN = 2, 2048, 512, 16, 2048
DH = D // HEADS
TOKENS = B * L
CH = 512
CHUNKS = TOKENS // CH
CPB = L // CH
KT = D // P
HG = P // DH
GROUPS = HEADS // HG
EPS = 1e-6
SCALE = 1.0 / float(DH) ** 0.5
PASSES = ((0, 0), (0, 1), (1, 0))
NORM = 3 + KT


class Rig:

    def __init__(self, nc, ctx, tag):
        self.nc, self.ctx, self.tag = nc, ctx, tag

    def sb(self, name, shape, dt=F32):
        return self.ctx.enter_context(self.nc.sbuf_tensor(f"{self.tag}_{name}", shape, dt))

    def ps(self, name, shape, dt=F32):
        return self.ctx.enter_context(self.nc.psum_tensor(f"{self.tag}_{name}", shape, dt))

    def sem(self, name):
        return self.ctx.enter_context(self.nc.semaphore(f"{self.tag}_{name}"))


def project(nc, xT, cT, wT, modT, mod_bias, ones_in, qk_scr, v_scr, mod):
    QK = 2 * GROUPS
    TILES = QK + CH // P
    BANKS = 6
    SLOTS = 4
    VSLOTS = 2
    with ExitStack() as ctx:
        rig = Rig(nc, ctx, "p1")
        w_raw = rig.sb("w_raw", [P, 3, KT, D])
        w_part = rig.sb("w_part", [P, 2, 3, KT, D], F32R)
        mod_w = rig.sb("mod_w", [P, 4, D])
        cond = rig.sb("cond", [P, B])
        bias = rig.sb("bias", [P, B, 4, KT])
        gb = rig.sb("gb", [P, 2, KT])
        ones = rig.sb("ones", [P, P])
        xc = rig.sb("xc", [P, 2, KT, CH])
        sq = rig.sb("sq", [P, KT, CH])
        rms = rig.sb("rms", [P, CH])
        inv = rig.sb("inv", [P, CH])
        h = rig.sb("h", [P, 2, 2, KT, CH], F32R)
        out_qk = rig.sb("out_qk", [P, SLOTS, 2, CH])
        out_v = rig.sb("out_v", [P, VSLOTS, D])
        tile = rig.ps("tile", [P, BANKS, CH])
        ss = rig.ps("ss", [P, CH])
        mod_ps = rig.ps("mod_ps", [P, B, 4, KT])

        consts_in = rig.sem("consts_in")
        weights_in = rig.sem("weights_in")
        weight_hi = rig.sem("weight_hi")
        weights_split = rig.sem("weights_split")
        mod_sums = rig.sem("mod_sums")
        mod_ready = rig.sem("mod_ready")
        x_in = [rig.sem(f"x_in{i}") for i in range(2)]
        sq_ready = rig.sem("sq_ready")
        sq_halved = rig.sem("sq_halved")
        sq_summed = rig.sem("sq_summed")
        ss_ready = rig.sem("ss_ready")
        rms_ready = rig.sem("rms_ready")
        norm_step = rig.sem("norm_step")
        h_hi = rig.sem("h_hi")
        h_ready = rig.sem("h_ready")
        tile_ready = rig.sem("tile_ready")
        tile_hi = rig.sem("tile_hi")
        tile_free = rig.sem("tile_free")
        qk_stored = [rig.sem(f"qk_stored{i}") for i in range(SLOTS)]
        v_stored = [rig.sem(f"v_stored{i}") for i in range(VSLOTS)]

        with nc.Block() as block:

            @block.gpsimd
            def _(pool):
                def load_x(c, par):
                    pool.dma_start(xc[:, par, :, :], xT[:, c, :, :].rearrange("k p t -> p k t")
                                   ).then_inc(x_in[par], 16)

                load_x(0, 0)
                pool.dma_start(ones[:, :], ones_in[:, :]).then_inc(consts_in, 16)
                pool.dma_start(cond[:, :], cT[:, :]).then_inc(consts_in, 16)
                pool.dma_start(bias[:, :, :, :], mod_bias[:, :, :, :]).then_inc(consts_in, 16)
                pool.dma_start(mod_w[:, :, :], modT[:, :, :]).then_inc(consts_in, 16)
                load_x(1, 1)
                for j in range(3):
                    pool.wait_ge(weight_hi, j + 1)
                    pool.tensor_tensor(w_part[:, 1, j, :, :], w_raw[:, j, :, :],
                                       w_part[:, 0, j, :, :].bitcast(F32), ALU.subtract
                                       ).then_inc(weights_split, 1)
                with pool.Fori(1, CHUNKS // 2) as it:
                    for par in range(2):
                        c = it * 2 + par
                        pool.wait_ge(h_ready, c - 1)
                        load_x(c, par)

            @block.sync
            def _(sp):
                for s in range(SLOTS):
                    sp.sem_inc(qk_stored[s], 32)
                for s in range(VSLOTS):
                    sp.sem_inc(v_stored[s], 16)
                for j in range(3):
                    sp.dma_start(w_raw[:, j, :, :], wT[j].rearrange("(k p) n -> p k n", p=P)
                                 ).then_inc(weights_in, 16)
                with sp.Fori(0, CHUNKS) as c:
                    for k in range(TILES):
                        sp.wait_ge(tile_free, c * TILES + BANKS + k + 1)
                        if k < QK:
                            for part in range(2):
                                sp.dma_start(qk_scr[k % 2, part, k // 2, c // CPB, c % CPB, :, :],
                                             out_qk[:, k % SLOTS, part, :]
                                             ).then_inc(qk_stored[k % SLOTS], 16)
                        else:
                            j = k - QK
                            sp.dma_start(v_scr[c // CPB, c % CPB * (CH // P) + j, :, :],
                                         out_v[:, j % VSLOTS, :]).then_inc(v_stored[j % VSLOTS], 16)
                for s in range(SLOTS):
                    sp.wait_ge(qk_stored[s], 32 * (QK // SLOTS) * CHUNKS + 32)
                for s in range(VSLOTS):
                    sp.wait_ge(v_stored[s], 16 * (TILES - QK) // VSLOTS * CHUNKS + 16)

            @block.scalar
            def _(act):
                def square(c, par, x_count):
                    act.wait_ge(x_in[par], x_count)
                    act.wait_ge(ss_ready, c)
                    act.activation(sq[:, :, :], xc[:, par, :, :], ACT.Square).then_inc(sq_ready, 1)

                def root(c):
                    act.wait_ge(ss_ready, c + 1)
                    act.activation(rms[:, :], ss[:, :], ACT.Sqrt, scale=1.0 / D, bias=EPS
                                   ).then_inc(rms_ready, 1)

                def norm_hi(c, par):
                    act.wait_ge(norm_step, (c + 1) * NORM)
                    act.activation(h[:, par, 0, :, :], xc[:, par, :, :], ACT.Copy
                                   ).then_inc(h_hi, 1)

                def chunk(c, par, x_count, norm_next):
                    if norm_next:
                        square(c + 1, 1 - par, x_count)
                    for k in range(QK):
                        act.wait_ge(tile_ready, c * TILES + k + 1)
                        act.wait_ge(qk_stored[k % SLOTS],
                                    c * (32 * (QK // SLOTS)) + 32 * (k // SLOTS) + 32)
                        act.activation(out_qk[:, k % SLOTS, 0, :].bitcast(F32R),
                                       tile[:, k % BANKS, :], ACT.Copy).then_inc(tile_hi, 1)
                        if norm_next and k == 3:
                            root(c + 1)
                    if norm_next:
                        norm_hi(c + 1, 1 - par)

                act.wait_ge(x_in[0], 16)
                act.activation(sq[:, :, :], xc[:, 0, :, :], ACT.Square).then_inc(sq_ready, 1)
                act.wait_ge(weights_in, 48)
                for j in range(3):
                    act.activation(w_part[:, 0, j, :, :], w_raw[:, j, :, :], ACT.Copy
                                   ).then_inc(weight_hi, 1)
                root(0)
                norm_hi(0, 0)
                with act.Fori(0, CHUNKS // 2 - 1) as it:
                    chunk(it * 2, 0, it * 16 + 16, True)
                    chunk(it * 2 + 1, 1, it * 16 + 32, True)
                chunk(CHUNKS - 2, 0, 16 * (CHUNKS // 2), True)
                chunk(CHUNKS - 1, 1, None, False)

            @block.vector
            def _(dve):
                dve.sem_inc(tile_free, BANKS)

                def sum_tiles(c):
                    dve.wait_ge(sq_ready, c + 1)
                    dve.tensor_tensor(sq[:, 0:2, :], sq[:, 0:2, :], sq[:, 2:4, :], ALU.add
                                      ).then_inc(sq_halved, 1)
                    dve.wait_ge(sq_halved, c + 1)
                    dve.tensor_tensor(sq[:, 0, :], sq[:, 0, :], sq[:, 1, :], ALU.add
                                      ).then_inc(sq_summed, 1)

                def norm(c, par, first):
                    done = c * NORM
                    dve.wait_ge(rms_ready, c + 1)
                    if not first:
                        dve.wait_ge(norm_step, done)
                    dve.reciprocal(inv[:, :], rms[:, :]).then_inc(norm_step, 1)
                    dve.wait_ge(norm_step, done + 1)
                    dve.tensor_tensor(xc[:, par, :, :], xc[:, par, :, :],
                                      inv[:, :].unsqueeze(1).broadcast_to([P, KT, CH]),
                                      ALU.mult).then_inc(norm_step, 1)
                    if first:
                        dve.wait_ge(mod_sums, 1)
                        dve.tensor_tensor(mod[:, :, :, :], mod_ps[:, :, :, :], bias[:, :, :, :],
                                          ALU.add).then_inc(mod_ready, 1)
                        dve.wait_ge(mod_ready, 1)
                    dve.tensor_scalar(gb[:, :, :], mod[:, c // CPB, 0:2, :], 1.0, None, ALU.mult
                                      ).then_inc(norm_step, 1)
                    dve.wait_ge(norm_step, done + 3)
                    for k in range(KT):
                        dve.tensor_scalar(xc[:, par, k, :], xc[:, par, k, :], gb[:, 0, k:k + 1],
                                          gb[:, 1, k:k + 1], ALU.mult, ALU.add
                                          ).then_inc(norm_step, 1)

                def norm_lo(c, par):
                    dve.wait_ge(h_hi, c + 1)
                    dve.tensor_tensor(h[:, par, 1, :, :], xc[:, par, :, :],
                                      h[:, par, 0, :, :].bitcast(F32), ALU.subtract
                                      ).then_inc(h_ready, 1)

                def chunk(c, par, norm_next):
                    for k in range(QK):
                        dve.wait_ge(tile_hi, c * QK + k + 1)
                        dve.tensor_tensor(out_qk[:, k % SLOTS, 1, :].bitcast(F32R),
                                          tile[:, k % BANKS, :], out_qk[:, k % SLOTS, 0, :],
                                          ALU.subtract).then_inc(tile_free, 1)
                        if norm_next and k == 0:
                            sum_tiles(c + 1)
                        if norm_next and k == 3:
                            norm(c + 1, 1 - par, False)
                    if norm_next:
                        norm_lo(c + 1, 1 - par)
                    for k in range(QK, TILES):
                        j = k - QK
                        dve.wait_ge(tile_ready, c * TILES + k + 1)
                        dve.wait_ge(v_stored[j % VSLOTS],
                                    c * (16 * (TILES - QK) // VSLOTS) + 16 * (j // VSLOTS) + 16)
                        dve.tensor_copy(out_v[:, j % VSLOTS, :], tile[:, k % BANKS, :]
                                        ).then_inc(tile_free, 1)

                sum_tiles(0)
                norm(0, 0, True)
                norm_lo(0, 0)
                with dve.Fori(0, CHUNKS // 2 - 1) as it:
                    chunk(it * 2, 0, True)
                    chunk(it * 2 + 1, 1, True)
                chunk(CHUNKS - 2, 0, True)
                chunk(CHUNKS - 1, 1, False)

            @block.tensor
            def _(pe):
                def sum_squares(c, first):
                    pe.wait_ge(sq_summed, c + 1)
                    if not first:
                        pe.wait_ge(rms_ready, c)
                    pe.matmul(ss[:, :], ones[:, :], sq[:, 0, :], start=True, stop=True
                              ).then_inc(ss_ready, 1)

                def chunk(c, par, norm_next):
                    pe.wait_ge(h_ready, c + 1)
                    for k in range(TILES):
                        pe.wait_ge(tile_free, c * TILES + k + 1)
                        n = 0
                        for kt in range(KT):
                            for stat, mov in PASSES:
                                if k < QK:
                                    g = k // 2
                                    lhs = w_part[:, stat, k % 2, kt, g * P:(g + 1) * P]
                                    rhs = h[:, par, mov, kt, :]
                                else:
                                    j = k - QK
                                    lhs = h[:, par, stat, kt, j * P:(j + 1) * P]
                                    rhs = w_part[:, mov, 2, kt, :]
                                mm = pe.matmul(tile[:, k % BANKS, :], lhs, rhs, start=(n == 0),
                                               stop=(n == 3 * KT - 1))
                                n += 1
                        mm.then_inc(tile_ready, 1)
                        if norm_next and k == 1:
                            sum_squares(c + 1, False)

                pe.wait_ge(consts_in, 64)
                sum_squares(0, True)
                for v in range(4):
                    for kt in range(KT):
                        mm = pe.matmul(mod_ps[:, :, v, kt], mod_w[:, v, kt * P:(kt + 1) * P],
                                       cond[:, :], start=True, stop=True)
                mm.then_inc(mod_sums, 1)
                pe.wait_ge(weights_split, 3)
                with pe.Fori(0, CHUNKS // 2 - 1) as it:
                    chunk(it * 2, 0, True)
                    chunk(it * 2 + 1, 1, True)
                chunk(CHUNKS - 2, 0, True)
                chunk(CHUNKS - 1, 1, False)


def attend(nc, qk_scr, v_scr, o_scr, ones_in, ident_in):
    QCHUNKS = B * GROUPS * CPB
    MT = L // P
    QT = CH // P
    KC = L // CH
    ROWS = 3 * DH
    AUG = ROWS + 2
    MAXMM = HG * QT * KC
    PER_STEP = MAXMM // MT
    FEW = 2
    TRANS_STEP = 13
    HEAD = PER_STEP * (MT - TRANS_STEP) + FEW
    REST = MAXMM - HEAD
    TRANS = REST + PER_STEP
    SLOTS = MAXMM + 2
    WIDE = 6
    SLAB = 4
    UPS = 2 * MT
    PAIRS = MT // 2
    with ExitStack() as ctx:
        rig = Rig(nc, ctx, "p2")
        q_stat = rig.sb("q_stat", [ROWS, HG, CH], F32R)
        q_mov = rig.sb("q_mov", [AUG, 2, HG, CH], F32R)
        k_mov = rig.sb("k_mov", [ROWS, 2, HG, L], F32R)
        k_stat = rig.sb("k_stat", [AUG, HG, L], F32R)
        v_next = rig.sb("v_next", [P, 2, MT, P])
        v_stat = rig.sb("v_stat", [P, MT, P])
        prob = rig.sb("prob", [P, SLAB, HG, CH])
        pair_sum = rig.sb("pair_sum", [P, 2, HG, CH])
        part = rig.sb("part", [P, HG * QT, KC])
        negmax = rig.sb("negmax", [P, HG * QT])
        negmax_part = rig.sb("negmax_part", [P, 2, HG * QT])
        rows = rig.sb("rows", [HG * QT, 2, P])
        o_sb = rig.sb("o_sb", [P, CH])
        den_sb = rig.sb("den_sb", [P, CH])
        ones = rig.sb("ones", [P, DH])
        ident = rig.sb("ident", [P, P])
        sT = rig.ps("sT", [P, 2, 2, CH])
        smax = rig.ps("smax", [P, 2, CH])
        o_ps = rig.ps("o_ps", [P, CH])
        den = rig.ps("den", [P, CH])

        consts_in = rig.sem("consts_in")
        aug_ones = rig.sem("aug_ones")
        k_in = [rig.sem(f"k_in{h}") for h in range(HG)]
        v_in = rig.sem("v_in")
        kv_tile = [rig.sem(f"kv_tile{i}") for i in range(MT)]
        q_in = [rig.sem(f"q_in{h}") for h in range(HG)]
        q_copied = rig.sem("q_copied")
        smax_ready = rig.sem("smax_ready")
        smax_free = rig.sem("smax_free")
        negmax_step = rig.sem("negmax_step")
        rows_in = rig.sem("rows_in")
        sT_ready = rig.sem("sT_ready")
        exp_done = rig.sem("exp_done")
        pv_done = rig.sem("pv_done")
        pair_added = rig.sem("pair_added")
        pair_used = rig.sem("pair_used")
        evacuated = rig.sem("evacuated")
        inverse = rig.sem("inverse")
        o_ready = rig.sem("o_ready")
        o_stored = rig.sem("o_stored")

        def score_bank(n, wide):
            if not wide:
                return smax[:, n % 2, :]
            n %= WIDE
            return smax[:, n, :] if n < 2 else sT[:, (n - 2) // 2, (n - 2) % 2, :]

        def slot(s, x):
            return s * SLOTS + (HEAD + x)

        with nc.Block() as block:

            @block.sync
            def _(sp):
                def load_k(bg, h):
                    g, b = bg % GROUPS, bg // GROUPS
                    for r, src in enumerate((0, 0, 1)):
                        sp.dma_start(
                            k_mov[r * DH:(r + 1) * DH, bg % 2, h, :].bitcast(F32)
                            .rearrange("p (c t) -> p c t", c=CPB),
                            qk_scr[1, src, g, b, :, h * DH:(h + 1) * DH, :]
                            .rearrange("c p t -> p c t")).then_inc(k_in[h], 16)

                def load_v(bg):
                    g, b = bg % GROUPS, bg // GROUPS
                    sp.dma_start(v_next[:, bg % 2, :, :],
                                 v_scr[b, :, :, bass.ds(g * P, P)].rearrange("i p d -> p i d")
                                 ).then_inc(v_in, 16)

                def load_q(bg, ch, h):
                    g, b = bg % GROUPS, bg // GROUPS
                    for r, src in ((1, 1), (0, 0), (2, 0)):
                        sp.dma_start(q_stat[r * DH:(r + 1) * DH, h, :].bitcast(F32),
                                     qk_scr[0, src, g, b, ch, h * DH:(h + 1) * DH, :]
                                     ).then_inc(q_in[h], 16)

                def next_q(bg, ch, h):
                    sp.wait_ge(smax_ready, slot(bg * CPB + ch, (h + 1) * QT * KC - HEAD))
                    if ch < CPB - 1:
                        load_q(bg, ch + 1, h)
                    else:
                        load_q(bg + 1, 0, h)

                def send_rows(s, x):
                    sp.wait_ge(smax_free, slot(s, x) + 4)
                    for r in range(2):
                        sp.dma_start(
                            q_mov[ROWS + r:ROWS + r + 1, s % 2, :, :].bitcast(F32)
                            .rearrange("o h (q t) -> o (h q) t", q=QT),
                            rows[:, r, :]).then_inc(rows_in, 16)

                def copy_tile(bg, i):
                    sp.wait_ge(pv_done, bg * (CPB * MT) + i + 1)
                    sp.dma_start(k_stat[0:ROWS, :, i * P:(i + 1) * P].bitcast(F32),
                                 k_mov[:, bg % 2, :, i * P:(i + 1) * P].bitcast(F32)
                                 ).then_inc(kv_tile[i], 16)
                    sp.dma_start(v_stat[:, i, :], v_next[:, bg % 2, i, :]).then_inc(kv_tile[i], 16)

                def group(bg, last):
                    for ch in range(CPB):
                        s = bg * CPB + ch
                        final = last and ch == CPB - 1
                        if ch == 0:
                            for h in range(HG):
                                sp.wait_ge(k_in[h], bg * 48 + 48)
                            sp.wait_ge(v_in, bg * 16 + 16)
                        if ch == 1 and not last:
                            for h in range(HG):
                                load_k(bg + 1, h)
                            load_v(bg + 1)
                        for i in range(MT):
                            if i % QT == 0 and not final:
                                next_q(bg, ch, i // QT)
                            if i == TRANS_STEP:
                                send_rows(s, REST if final else TRANS)
                            if ch == 0:
                                copy_tile(bg, i)

                for h in range(HG):
                    load_k(0, h)
                    load_q(0, 0, h)
                load_v(0)
                sp.dma_start(ones[:, :], ones_in[:, 0:DH]).then_inc(consts_in, 16)
                sp.dma_start(ident[:, :], ident_in[:, :]).then_inc(consts_in, 16)
                with sp.Fori(0, B * GROUPS - 1) as bg:
                    group(bg, False)
                group(B * GROUPS - 1, True)

            @block.gpsimd
            def _(pool):
                def copy_q(s, h, used):
                    pool.wait_ge(q_in[h], s * 48 + 48)
                    if used and h == 0:
                        pool.wait_ge(sT_ready, s * UPS - UPS)
                    pool.tensor_copy(q_mov[0:ROWS, s % 2, h, :],
                                     q_stat[:, h, :].bitcast(F32)).then_inc(q_copied, 1)

                def add_pair(c, j):
                    pool.wait_ge(exp_done, c * UPS + 4 * j + 6)
                    pool.wait_ge(pair_used, c * PAIRS + j + 1)
                    at = 2 * j % SLAB
                    pool.tensor_tensor(pair_sum[:, j % 2, :, :], prob[:, at, :, :],
                                       prob[:, at + 1, :, :], ALU.add).then_inc(pair_added, 1)

                def chunk(c, first, last):
                    if not last:
                        copy_q(c + 1, 0, not first)
                    if not first:
                        add_pair(c - 1, PAIRS - 1)
                    if not last:
                        for h in range(1, HG):
                            copy_q(c + 1, h, not first)
                    for j in range(PAIRS - 1):
                        add_pair(c, j)
                        if j == PAIRS - 3 and not first:
                            store_o(c - 1)

                def store_o(c):
                    pool.wait_ge(o_ready, c + 1)
                    pool.dma_start(o_scr[c // CPB % GROUPS, c // CPB // GROUPS, c % CPB, :, :],
                                   o_sb[:, :]).then_inc(o_stored, 16)

                pool.memset(k_stat[ROWS:AUG, :, :].bitcast(F32), 1.0).then_inc(aug_ones, 1)
                pool.sem_inc(pair_added, 2)
                for h in range(HG):
                    copy_q(0, h, False)
                chunk(0, True, False)
                with pool.Fori(1, QCHUNKS - 1) as c:
                    chunk(c, False, False)
                chunk(QCHUNKS - 1, False, True)
                add_pair(QCHUNKS - 1, PAIRS - 1)
                store_o(QCHUNKS - 1)
                pool.wait_ge(o_stored, 16 * QCHUNKS)

            @block.scalar
            def _(act):
                act.sem_inc(exp_done, 2)
                act.sem_inc(evacuated, 2)

                def chunk(c, first):
                    for n in range(UPS):
                        i = n // 2
                        act.wait_ge(sT_ready, c * UPS + n + 1)
                        if n % 2 == 0:
                            act.wait_ge(pv_done, c * MT + (MT - SLAB) + i + 1)
                            act.wait_ge(pair_added, c * PAIRS + i // 2 + 1)
                        act.activation(prob[:, i % SLAB, n % 2 * 2:n % 2 * 2 + 2, :],
                                       sT[:, n % 2, :, :], ACT.Exp, scale=SCALE
                                       ).then_inc(exp_done, 1)
                        if n == 5 and not first:
                            evacuate_denominators(c - 1)
                    if not first:
                        act.wait_ge(o_stored, c * 16)
                    act.wait_ge(pv_done, c * MT + 2 * MT)
                    act.activation(o_sb[:, :], o_ps[:, :], ACT.Copy).then_inc(evacuated, 1)

                def evacuate_denominators(c):
                    act.wait_ge(pair_used, c * PAIRS + PAIRS + 2)
                    act.activation(den_sb[:, :], den[:, :], ACT.Copy).then_inc(evacuated, 1)

                chunk(0, True)
                with act.Fori(1, QCHUNKS) as c:
                    chunk(c, False)
                evacuate_denominators(QCHUNKS - 1)

            @block.vector
            def _(dve):
                OUT_AT = (17, 25, 33, 41, 49)

                def reduce(at, k, x, wide=False):
                    dve.wait_ge(smax_ready, at + 1)
                    dve.tensor_reduce(part[:, k // KC, k % KC:k % KC + 1], score_bank(x, wide),
                                      AX_X, ALU.max).then_inc(smax_free, 1)

                def output_step(c, n):
                    if n < QT:
                        if n == 0:
                            dve.wait_ge(evacuated, c * 2 + 4)
                        cols = slice(n * P, (n + 1) * P)
                        dve.reciprocal(den_sb[:, cols], den_sb[:, cols]).then_inc(inverse, 1)
                    else:
                        dve.wait_ge(inverse, c * QT + QT)
                        dve.tensor_tensor(o_sb[:, :], o_sb[:, :], den_sb[:, :], ALU.mult
                                          ).then_inc(o_ready, 1)

                def maxima(s, first, with_next, out_chunk):
                    for x in range(REST):
                        if out_chunk is not None and x in OUT_AT:
                            output_step(out_chunk, OUT_AT.index(x))
                        reduce(slot(s, x), HEAD + x, HEAD + x, first)
                    dve.wait_ge(smax_free, slot(s, REST) + 2)
                    dve.tensor_reduce(negmax[:, :], part[:, :, :], AX_X, ALU.max, negate=True
                                      ).then_inc(negmax_step, 1)
                    dve.wait_ge(negmax_step, s * 3 + 1)
                    dve.tensor_copy(negmax_part[:, 0, :].bitcast(F32R), negmax[:, :]
                                    ).then_inc(negmax_step, 1)
                    dve.wait_ge(negmax_step, s * 3 + 2)
                    dve.tensor_tensor(negmax_part[:, 1, :], negmax[:, :],
                                      negmax_part[:, 0, :], ALU.subtract).then_inc(negmax_step, 1)
                    trans = TRANS if with_next else REST
                    if with_next:
                        for k in range(PER_STEP):
                            reduce(slot(s, REST + k), k, k)
                    if not first:
                        dve.wait_ge(rows_in, s * 32)
                    for r in range(2):
                        dve.wait_ge(smax_ready, slot(s, trans) + r + 1)
                        dve.tensor_copy(rows[:, r, :], smax[0:HG * QT, r, 0:P]
                                        ).then_inc(smax_free, 1)
                    if with_next:
                        for k in range(PER_STEP, HEAD):
                            reduce(slot(s, REST + 2 + k), k, k)

                dve.sem_inc(smax_free, 2)
                for k in range(HEAD):
                    reduce(k, k, k, True)
                maxima(0, True, True, None)
                maxima(1, False, True, None)
                with dve.Fori(2, QCHUNKS - 1) as s:
                    maxima(s, False, True, s - 2)
                maxima(QCHUNKS - 1, False, False, QCHUNKS - 3)
                for c in (QCHUNKS - 2, QCHUNKS - 1):
                    for n in range(QT + 1):
                        output_step(c, n)

            @block.tensor
            def _(pe):
                def scores_T(c, i, h):
                    pair = h // 2
                    if h % 2 == 0:
                        pe.wait_ge(exp_done, c * UPS + 2 * i + pair + 1)
                    mm = pe.matmul(sT[:, pair, h % 2, :], k_stat[:, h, i * P:(i + 1) * P],
                                   q_mov[:, c % 2, h, :], start=True, stop=True)
                    if h % 2 == 1:
                        mm.then_inc(sT_ready, 1)

                def scores_for_max(s, k, at, n, wide=False):
                    h, q, kc = k // (QT * KC), k // KC % QT, k % KC
                    if k % (QT * KC) == 0:
                        pe.wait_ge(k_in[h], s // CPB * 48 + 48)
                        pe.wait_ge(q_in[h], s * 48 + 48)
                    if k % (QT * KC) == QT * KC - 1:
                        pe.wait_ge(q_copied, s * HG + h + 1)
                    if not wide:
                        pe.wait_ge(smax_free, at + 1)
                    elif n >= WIDE:
                        pe.wait_ge(smax_free, n - WIDE + 3)
                    pe.matmul(score_bank(n, wide), q_stat[:, h, q * P:(q + 1) * P],
                              k_mov[:, s // CPB % 2, h, kc * CH:(kc + 1) * CH],
                              start=True, stop=True).then_inc(smax_ready, 1)

                def transpose_max(s, x):
                    pe.wait_ge(negmax_step, s * 3 + 3)
                    for r in range(2):
                        pe.wait_ge(smax_free, slot(s, x) + r + 1)
                        pe.transpose(smax[0:HG * QT, r, 0:P], negmax_part[:, r, :], ident[:, :]
                                     ).then_inc(smax_ready, 1)

                def columns(out, stat, mov, start, stop):
                    for h in range(HG):
                        cols = slice(h * DH, (h + 1) * DH)
                        mm = pe.matmul(out[cols, :], stat(cols), mov[:, h, :], start=start,
                                       stop=stop)
                    return mm

                def times_v(c, i):
                    pe.wait_ge(exp_done, c * UPS + 2 + 2 * i + 2)
                    if i == 0:
                        pe.wait_ge(evacuated, c * 2 + 1)
                    columns(o_ps, lambda cols: v_stat[:, i, cols], prob[:, i % SLAB, :, :],
                            i == 0, i == MT - 1).then_inc(pv_done, 1)

                def denominators(c, j):
                    pe.wait_ge(pair_added, c * PAIRS + j + 3)
                    if j == 0:
                        pe.wait_ge(evacuated, c * 2 + 2)
                    columns(den, lambda cols: ones[:, :], pair_sum[:, j % 2, :, :], j == 0,
                            j == PAIRS - 1).then_inc(pair_used, 1)

                def body(s, with_max, with_softmax, with_next, with_last=True):
                    if with_softmax:
                        c = s - 1
                        pe.wait_ge(rows_in, c * 32 + 32)
                        pe.wait_ge(q_copied, c * HG + HG)
                    x = 0

                    def for_max(count=1):
                        nonlocal x
                        for _ in range(count):
                            if x < REST:
                                if with_max:
                                    scores_for_max(s, HEAD + x, slot(s, x), HEAD + x,
                                                   not with_softmax)
                            elif with_next:
                                at = x if x < TRANS else x + 2
                                scores_for_max(s + 1, x - REST, slot(s, at), x)
                            x += 1

                    for i in range(MT):
                        pairs = i % 2 == 0 and (i >= 4 or i == 2 and with_softmax and with_last)
                        if i > 0:
                            for_max()
                        if with_softmax:
                            pe.wait_ge(kv_tile[i], (s - 1) // CPB * 32 + 32)
                        for h in range(HG):
                            if with_softmax:
                                scores_T(c, i, h)
                            if h == 1 if pairs or i == 0 else h in (0, 2):
                                for_max()
                        for_max()
                        if with_softmax and i > 0:
                            times_v(c, i - 1)
                        if pairs:
                            for_max()
                            if with_softmax and i == 2:
                                denominators(c - 1, PAIRS - 1)
                            elif with_softmax:
                                denominators(c, i // 2 - 2)
                        if with_max and i == TRANS_STEP:
                            transpose_max(s, TRANS if with_next else REST)
                    if with_softmax:
                        denominators(c, PAIRS - 2)
                    for_max()
                    if with_softmax:
                        times_v(c, MT - 1)
                    for_max()

                pe.sem_inc(pv_done, MT)
                pe.sem_inc(pair_used, 2)
                for k in range(HEAD):
                    scores_for_max(0, k, k, k, True)
                pe.wait_ge(consts_in, 32)
                body(0, True, False, True)
                pe.wait_ge(aug_ones, 1)
                body(1, True, True, True, with_last=False)
                with pe.Fori(2, QCHUNKS - 1) as s:
                    body(s, True, True, True)
                body(QCHUNKS - 1, True, True, False)
                body(QCHUNKS, False, True, False)
                denominators(QCHUNKS - 1, PAIRS - 1)


def feed(nc, xT, woT, w_blocks, ones_in, o_scr, out, mod):
    HB = 2 * P
    NB = HIDDEN // HB
    HT = HB // P
    WIDTH = 2 * KT * HB + HT * D
    TPB = CPB * HT
    ITER = 2 * TPB
    TOKENS0 = 2 * TPB
    with ExitStack() as ctx:
        rig = Rig(nc, ctx, "p3")
        h = rig.sb("h", [P, 2, CPB, KT, CH], F32R)
        y = rig.sb("y", [P, CPB, KT, CH])
        wo_part = rig.sb("wo_part", [P, 2, KT, D], F32R)
        scratch = rig.sb("scratch", [P, 2 * KT * CH])
        act_sb = rig.sb("act_sb", [P, 2, CH])
        w_part = rig.sb("w_part", [P, 2, 2, WIDTH], F32R)
        o_raw = rig.sb("o_raw", [P, KT, CH])
        x1_even = rig.sb("x1_even", [P, KT, CH])
        rms = rig.sb("rms", [P, CH])
        gb = rig.sb("gb", [P, 2, KT])
        ones = rig.sb("ones", [P, P])
        a = rig.sb("a", [P, 2, 2, CH], F32R)
        bank = rig.ps("bank", [P, 8, CH])
        w_raw = scratch[:, 0:WIDTH]
        sq = scratch[:, 0:KT * CH].rearrange("p (k t) -> p k t", k=KT)
        x1_odd = scratch[:, KT * CH:2 * KT * CH].rearrange("p (k t) -> p k t", k=KT)
        x1s = (x1_even[:, :, :], x1_odd)
        wo_raw = scratch[:, 0:KT * D].rearrange("p (k n) -> p k n", k=KT)

        def gate_up(parity, part, which, kt, ht):
            at = (which * KT + kt) * HB + ht * P
            return w_part[:, parity, part, at:at + P]

        def down(parity, part, ht, f):
            at = 2 * KT * HB + ht * D + f * P
            return w_part[:, parity, part, at:at + P]

        wo_in = rig.sem("wo_in")
        ones_loaded = rig.sem("ones_loaded")
        wo_hi = rig.sem("wo_hi")
        wo_split = rig.sem("wo_split")
        x_in = [rig.sem(f"x_in{c}") for c in range(CPB)]
        o_in = rig.sem("o_in")
        o_hi = rig.sem("o_hi")
        o_split = rig.sem("o_split")
        proj_ready = rig.sem("proj_ready")
        x1_ready = rig.sem("x1_ready")
        y_init = rig.sem("y_init")
        sq_ready = rig.sem("sq_ready")
        sq_summed = rig.sem("sq_summed")
        gb_ready = rig.sem("gb_ready")
        ss_ready = rig.sem("ss_ready")
        rms_ready = rig.sem("rms_ready")
        inv_ready = rig.sem("inv_ready")
        scaled = rig.sem("scaled")
        normed = rig.sem("normed")
        h_hi = rig.sem("h_hi")
        h_ready = rig.sem("h_ready")
        w_in = rig.sem("w_in")
        w_hi = rig.sem("w_hi")
        w_split = rig.sem("w_split")
        gu_ready = rig.sem("gu_ready")
        silu_done = rig.sem("silu_done")
        gu_free = rig.sem("gu_free")
        a_hi = rig.sem("a_hi")
        a_ready = rig.sem("a_ready")
        down_done = rig.sem("down_done")
        y_added = rig.sem("y_added")
        y_stored = [rig.sem(f"y_stored{c}") for c in range(CPB)]

        with nc.Block() as block:

            @block.sync
            def _(sp):
                def load_o(b, ch):
                    if b + ch > 0:
                        sp.wait_ge(o_split, b * CPB + ch)
                    sp.dma_start(o_raw[:, :, :], o_scr[:, b, ch, :, :]
                                 .rearrange("g p t -> p g t")).then_inc(o_in, 16)

                def load_x(b, ch):
                    sp.dma_start(y[:, ch, :, :], xT[:, b * CPB + ch, :, :]
                                 .rearrange("k p t -> p k t")).then_inc(x_in[ch], 16)

                def load_w(w):
                    sp.dma_start(w_raw, w_blocks[w % NB, :, :]).then_inc(w_in, 16)

                def batch(b, last):
                    for ch in range(1, CPB):
                        load_o(b, ch)
                    sp.wait_ge(y_init, b * CPB + CPB)
                    sp.wait_ge(h_ready, b * CPB + CPB)
                    load_w(b * NB + 1)
                    with sp.Fori(2, NB if last else NB + 1) as j:
                        sp.wait_ge(w_split, j + b * NB)
                        load_w(j + b * NB)
                    if not last:
                        load_o(b + 1, 0)
                    for ch in range(CPB):
                        sp.wait_ge(y_added, CPB + (b * NB + NB - 1) * CPB + ch + 1)
                        sp.dma_start(out[:, b * CPB + ch, :, :].rearrange("k p t -> p k t"),
                                     y[:, ch, :, :]).then_inc(y_stored[ch], 16)
                        if not last:
                            sp.wait_ge(y_stored[ch], b * 16 + 16)
                            load_x(b + 1, ch)

                sp.dma_start(wo_raw, woT.rearrange("(k p) n -> p k n", p=P)
                             ).then_inc(wo_in, 16)
                load_o(0, 0)
                sp.dma_start(ones[:, :], ones_in[:, :]).then_inc(ones_loaded, 16)
                for ch in range(CPB):
                    load_x(0, ch)
                sp.wait_ge(wo_split, 1)
                load_w(0)
                for b in range(B):
                    batch(b, b == B - 1)
                for ch in range(CPB):
                    sp.wait_ge(y_stored[ch], B * 16)

            @block.gpsimd
            def _(pool):
                def split(w):
                    pool.wait_ge(w_in, w * 16 + 16)
                    pool.wait_ge(down_done, w * TPB + TPB)
                    pool.tensor_copy(w_part[:, w % 2, 0, :], w_raw).then_inc(w_hi, 1)
                    pool.wait_ge(w_hi, w + 1)
                    pool.tensor_tensor(w_part[:, w % 2, 1, :], w_raw,
                                       w_part[:, w % 2, 0, :].bitcast(F32), ALU.subtract
                                       ).then_inc(w_split, 1)

                for b in range(B):
                    split(b * NB)
                    for ch in range(CPB):
                        pool.wait_ge(x1_ready, b * CPB + ch + 1)
                        pool.tensor_tensor(y[:, ch, :, :], y[:, ch, :, :], x1s[ch % 2], ALU.add
                                           ).then_inc(y_init, 1)
                    with pool.Fori(1, NB) as j:
                        split(b * NB + j)

            @block.scalar
            def _(act):
                def o_hi_part(b, ch):
                    act.wait_ge(o_in, (b * CPB + ch) * 16 + 16)
                    act.activation(h[:, 0, ch, :, :], o_raw[:, :, :], ACT.Copy).then_inc(o_hi, 1)

                def square(b, ch):
                    act.wait_ge(x1_ready, b * CPB + ch + 1)
                    act.activation(sq, x1s[ch % 2], ACT.Square).then_inc(sq_ready, 1)

                def root(b, ch):
                    act.wait_ge(ss_ready, b * CPB + ch + 1)
                    act.activation(rms[:, :], bank[:, 4 * (ch % 2), :], ACT.Sqrt,
                                   scale=1.0 / D, bias=EPS).then_inc(rms_ready, 1)

                def norm_hi(b, ch):
                    c, x1 = b * CPB + ch, x1s[ch % 2]
                    act.wait_ge(gb_ready, b + 1)
                    act.wait_ge(scaled, c + 1)
                    for k in range(KT):
                        act.activation(x1[:, k, :], x1[:, k, :], ACT.Identity,
                                       scale=gb[:, 0, k:k + 1], bias=gb[:, 1, k:k + 1]
                                       ).then_inc(normed, 1)
                    act.wait_ge(normed, c * KT + KT)
                    act.activation(h[:, 0, ch, :, :], x1, ACT.Copy).then_inc(h_hi, 1)

                def swiglu(b, hp, first):
                    done = (b * (NB // 2) + hp) * ITER
                    if first:
                        root(b, CPB - 1)
                    for t in range(ITER):
                        act.wait_ge(gu_ready, done + t + 1)
                        act.wait_ge(a_ready, done + t + 1)
                        act.activation(act_sb[:, t % 2, :], bank[:, 2 * (t % 2), :], ACT.Silu
                                       ).then_inc(silu_done, 1)
                        act.wait_ge(gu_free, done + t + 3)
                        act.wait_ge(down_done, done + TOKENS0 + t - 1)
                        act.activation(a[:, t % 2, 0, :], act_sb[:, t % 2, :], ACT.Copy
                                       ).then_inc(a_hi, 1)
                        if first and t == 2:
                            norm_hi(b, CPB - 1)

                act.wait_ge(wo_in, 16)
                act.activation(wo_part[:, 0, :, :], wo_raw, ACT.Copy).then_inc(wo_hi, 1)
                with act.Fori(0, B) as b:
                    o_hi_part(b, 0)
                    o_hi_part(b, 1)
                    act.wait_ge(w_split, b * NB + 1)
                    square(b, 0)
                    for ch in range(CPB - 1):
                        if ch + 2 < CPB:
                            o_hi_part(b, ch + 2)
                        root(b, ch)
                        square(b, ch + 1)
                        norm_hi(b, ch)
                    swiglu(b, 0, True)
                    with act.Fori(1, NB // 2) as hp:
                        swiglu(b, hp, False)

            @block.vector
            def _(dve):
                dve.sem_inc(y_added, CPB)
                dve.sem_inc(gu_free, 2)
                dve.sem_inc(a_ready, 2)

                def o_lo_part(b, ch):
                    dve.wait_ge(o_hi, b * CPB + ch + 1)
                    dve.tensor_tensor(h[:, 1, ch, :, :], o_raw[:, :, :],
                                      h[:, 0, ch, :, :].bitcast(F32), ALU.subtract
                                      ).then_inc(o_split, 1)

                def add_y(done, t):
                    dve.wait_ge(down_done, done + TOKENS0 + t + 1)
                    ch = t // HT % CPB
                    dve.tensor_tensor(y[:, ch, :, :], y[:, ch, :, :], bank[:, 4:8, :], ALU.add
                                      ).then_inc(y_added, 1)

                dve.wait_ge(wo_hi, 1)
                dve.tensor_tensor(wo_part[:, 1, :, :], wo_raw, wo_part[:, 0, :, :].bitcast(F32),
                                  ALU.subtract).then_inc(wo_split, 1)
                with dve.Fori(0, B) as b:
                    def h_lo_part(ch):
                        dve.wait_ge(h_hi, b * CPB + ch + 1)
                        dve.tensor_tensor(h[:, 1, ch, :, :], x1s[ch % 2],
                                          h[:, 0, ch, :, :].bitcast(F32), ALU.subtract
                                          ).then_inc(h_ready, 1)

                    def add_x(ch):
                        c = b * CPB + ch
                        dve.wait_ge(proj_ready, c + 1)
                        dve.wait_ge(x_in[ch], b * 16 + 16)
                        if ch > 1:
                            dve.wait_ge(y_init, c - 1)
                            dve.wait_ge(h_ready, c - 1)
                        dve.tensor_tensor(x1s[ch % 2], bank[:, 4 * (ch % 2):4 * (ch % 2) + 4, :],
                                          y[:, ch, :, :], ALU.add).then_inc(x1_ready, 1)

                    def sum_squares(ch):
                        dve.wait_ge(sq_ready, b * CPB + ch + 1)
                        dve.tensor_tensor(sq[:, 0:2, :], sq[:, 0:2, :], sq[:, 2:4, :], ALU.add
                                          ).then_inc(sq_summed, 1)

                    def invert(ch):
                        dve.wait_ge(rms_ready, b * CPB + ch + 1)
                        dve.reciprocal(rms[:, :], rms[:, :]).then_inc(inv_ready, 1)

                    def scale(ch):
                        c, x1 = b * CPB + ch, x1s[ch % 2]
                        dve.wait_ge(inv_ready, c + 1)
                        dve.wait_ge(y_init, c + 1)
                        dve.tensor_tensor(x1, x1, rms[:, :].unsqueeze(1).broadcast_to([P, KT, CH]),
                                          ALU.mult).then_inc(scaled, 1)

                    def swiglu(hp, first):
                        done = (b * (NB // 2) + hp) * ITER
                        dve.wait_ge(y_added, (b * (NB // 2) + hp) * (ITER // HT) + CPB)
                        for t in range(ITER):
                            dve.wait_ge(silu_done, done + t + 1)
                            dve.tensor_tensor(act_sb[:, t % 2, :], bank[:, 2 * (t % 2) + 1, :],
                                              act_sb[:, t % 2, :], ALU.mult).then_inc(gu_free, 1)
                            dve.wait_ge(a_hi, done + t + 1)
                            dve.tensor_tensor(a[:, t % 2, 1, :], act_sb[:, t % 2, :],
                                              a[:, t % 2, 0, :].bitcast(F32), ALU.subtract
                                              ).then_inc(a_ready, 1)
                            if t >= 2 and t % 2 == 0:
                                add_y(done, t - 1)
                            if first and t == 1:
                                invert(CPB - 1)
                                scale(CPB - 1)
                            if first and t == 3:
                                h_lo_part(CPB - 1)
                        add_y(done, ITER - 1)

                    o_lo_part(b, 0)
                    dve.tensor_scalar(gb[:, :, :], mod[:, b, 2:4, :], 1.0, None, ALU.mult
                                      ).then_inc(gb_ready, 1)
                    o_lo_part(b, 1)
                    add_x(0)
                    sum_squares(0)
                    for ch in range(CPB - 1):
                        if ch + 2 < CPB:
                            o_lo_part(b, ch + 2)
                        if ch > 0:
                            h_lo_part(ch - 1)
                        invert(ch)
                        add_x(ch + 1)
                        scale(ch)
                        sum_squares(ch + 1)
                    h_lo_part(CPB - 2)
                    swiglu(0, True)
                    with dve.Fori(1, NB // 2) as hp:
                        swiglu(hp, False)

            @block.tensor
            def _(pe):
                pe.sem_inc(down_done, TOKENS0)

                def sum_squares(b, ch):
                    c = b * CPB + ch
                    pe.wait_ge(sq_summed, c + 1)
                    pe.wait_ge(x1_ready, c + 1)
                    for k in range(2):
                        mm = pe.matmul(bank[:, 4 * (ch % 2), :], ones[:, :], sq[:, k, :],
                                       start=(k == 0), stop=(k == 1))
                    mm.then_inc(ss_ready, 1)

                def project_o(b, ch):
                    c, at = b * CPB + ch, 4 * (ch % 2)
                    pe.wait_ge(o_split, c + 1)
                    if ch == 0:
                        pe.wait_ge(gu_free, b * (NB * TPB) + 2)
                    elif ch == 1:
                        pe.wait_ge(y_added, b * (NB * CPB) + CPB)
                    else:
                        pe.wait_ge(x1_ready, c - 1)
                    for f in (1, 2, 3, 0):
                        if f == 0 and ch > 0:
                            sum_squares(b, ch - 1)
                        if f == 0 and ch > 1:
                            pe.wait_ge(rms_ready, c - 1)
                        n = 0
                        for g in range(KT):
                            for stat, mov in PASSES:
                                mm = pe.matmul(bank[:, at + f, :],
                                               wo_part[:, stat, g, f * P:(f + 1) * P],
                                               h[:, mov, ch, g, :], start=(n == 0),
                                               stop=(n == 3 * KT - 1))
                                n += 1
                    mm.then_inc(proj_ready, 1)

                def tile(done, t):
                    parity, ch, ht = t // TPB, t // HT % CPB, t % HT
                    pe.wait_ge(gu_free, done + t + 1)
                    for which in range(2):
                        n = 0
                        for kt in range(KT):
                            for stat, mov in PASSES:
                                mm = pe.matmul(bank[:, 2 * (t % 2) + which, :],
                                               gate_up(parity, stat, which, kt, ht),
                                               h[:, mov, ch, kt, :], start=(n == 0),
                                               stop=(n == 3 * KT - 1))
                                n += 1
                    mm.then_inc(gu_ready, 1)

                def down_tile(done, t, added):
                    parity, ht = t // TPB, t % HT
                    pe.wait_ge(a_ready, done + t + 3)
                    if ht == 0:
                        pe.wait_ge(y_added, added + CPB + t // HT)
                    for f in range(KT):
                        for n, (stat, mov) in enumerate(PASSES):
                            mm = pe.matmul(bank[:, 4 + f, :], down(parity, stat, ht, f),
                                           a[:, t % 2, mov, :], start=(ht == 0 and n == 0),
                                           stop=(ht == HT - 1 and n == 2))
                    mm.then_inc(down_done, 1)

                def swiglu(b, hp, first):
                    done = (b * (NB // 2) + hp) * ITER
                    added = (b * (NB // 2) + hp) * (ITER // HT)
                    if first:
                        pe.wait_ge(x1_ready, b * CPB + CPB - 1)
                        pe.wait_ge(rms_ready, b * CPB + CPB - 1)
                    for t in range(ITER):
                        if t % TPB == 0:
                            pe.wait_ge(w_split, b * NB + hp * 2 + t // TPB + 1)
                        if first and t < TPB and t % HT == 0:
                            pe.wait_ge(h_ready, b * CPB + t // HT + 1)
                        tile(done, t)
                        if first and t == 1:
                            sum_squares(b, CPB - 1)
                            pe.wait_ge(rms_ready, b * CPB + CPB)
                        if t > 0:
                            down_tile(done, t - 1, added)
                    down_tile(done, ITER - 1, added)

                pe.wait_ge(ones_loaded, 16)
                pe.wait_ge(wo_split, 1)
                with pe.Fori(0, B) as b:
                    for ch in range(CPB):
                        project_o(b, ch)
                    swiglu(b, 0, True)
                    with pe.Fori(1, NB // 2) as hp:
                        swiglu(b, hp, False)


def build(nc, xT, cT, wT, modT, mod_bias, woT, w_blocks, ones_in, ident_in, out):
    qk_scr = nc.dram_tensor("qk_scr", (2, 2, GROUPS, B, CPB, P, CH), F32).ap()
    v_scr = nc.dram_tensor("v_scr", (B, L // P, P, D), F32).ap()
    o_scr = nc.dram_tensor("o_scr", (GROUPS, B, CPB, P, CH), F32).ap()
    with nc.sbuf_tensor("mod", [P, B, 4, KT], F32) as mod:
        project(nc, xT, cT, wT, modT, mod_bias, ones_in, qk_scr, v_scr, mod)
        attend(nc, qk_scr, v_scr, o_scr, ones_in, ident_in)
        feed(nc, xT, woT, w_blocks, ones_in, o_scr, out, mod)


def kernel(**inputs):
    import numpy as np
    import concourse.bacc as bacc
    from concourse import mybir as mb
    from concourse.bass_utils import run_bass_kernel_spmd as run

    def w(name):
        return np.asarray(inputs["L0_cond_" + name])

    def features_first(v):
        return v.reshape(CHUNKS, CH, KT, P).transpose(2, 0, 3, 1)

    def vector(name):
        return w(name).reshape(KT, P).T

    blocks, hb = 8, 256
    gate = w("gate_w").T.reshape(KT, P, blocks, hb).transpose(2, 1, 0, 3)
    hid = w("hid_w").T.reshape(KT, P, blocks, hb).transpose(2, 1, 0, 3)
    down = w("out_w").T.reshape(blocks, hb // P, P, D).transpose(0, 2, 1, 3)
    bias = np.stack([vector(n) for n in ("g1b", "b1b", "g2b", "b2b")], axis=1)
    arrays = {
        "xT": features_first(np.asarray(inputs["x"])),
        "cT": np.asarray(inputs["cond_256"]).T,
        "wT": np.stack([w(n).T for n in ("Wq", "Wk", "Wv")]),
        "modT": np.stack([w(n).T for n in ("g1w", "b1w", "g2w", "b2w")], axis=1),
        "mod_bias": np.stack([bias, bias], axis=1),
        "woT": w("Wo").T,
        "w_blocks": np.concatenate([v.reshape(blocks, P, -1) for v in (gate, hid, down)], axis=2),
        "ones": np.ones((P, P), np.float32),
        "ident": np.eye(P, dtype=np.float32),
    }
    nc = bacc.Bacc("TRN2", target_bir_lowering=False, num_devices=1)
    arrays = {f"in_{k}": np.ascontiguousarray(v) for k, v in arrays.items()}
    args = [nc.dram_tensor(k, v.shape, mb.dt.from_np(v.dtype), kind="ExternalInput").ap()
            for k, v in arrays.items()]
    out = nc.dram_tensor("out", (KT, CHUNKS, P, CH), F32, kind="ExternalOutput").ap()
    build(nc, *args, out)
    got = run(nc, [arrays], core_ids=[0]).results[0]["out"]
    return np.ascontiguousarray(got.transpose(1, 3, 0, 2)).reshape(B, L, D)
```
